# Optimizing a Trainium2 kernel written in Bass

```python
import numpy as np
import jax
import jax.numpy as jnp

def _softmax(x, axis=-1):
    return jax.nn.softmax(x, axis=axis)

def _gelu(x):
    return jax.nn.gelu(x, approximate=True)

def _silu(x):
    return jax.nn.silu(x)

def _sigmoid(x):
    return jax.nn.sigmoid(x)

def _layernorm(x, axis=-1, eps=1e-05):
    m = jnp.mean(x, axis=axis, keepdims=True)
    v = jnp.var(x, axis=axis, keepdims=True)
    return (x - m) / jnp.sqrt(v + eps)

def _scatter_add(tgt, idx, src, axis=0):
    return tgt.at[idx].add(src)

def _segment_sum(src, seg, n):
    return jax.ops.segment_sum(src, seg, n)
kernel_name = 'mk_recurrent_d2_jaxref_r4_105397'

def setup_inputs(seed: int=0):
    np.random.seed(seed)
    _w = jnp.asarray

    def _L0_attn_setup():
        import jax, jax.numpy as jnp
        import numpy as np
        B, N, C = (8, 1024, 256)
        key = jax.random.key(seed)
        k1, k2, k3 = jax.random.split(key, 3)
        x = jax.random.normal(k1, (B, N, C), dtype=jnp.float32)
        w_qkv = jax.random.normal(k2, (3 * C, C), dtype=jnp.float32) * C ** (-0.5)
        w_conv1 = jax.random.normal(k3, (C,), dtype=jnp.float32) * C ** (-0.5)
        return {'x': x, 'w_qkv': w_qkv, 'w_conv1': w_conv1}
    _L0_attn_in = _L0_attn_setup()

    def _L0_ffn_setup():
        import jax, jax.numpy as jnp
        import numpy as np
        E, D, F = (8, 256, 1024)
        LN_EPS = 1e-05
        key = jax.random.key(seed)
        k = jax.random.split(key, 8)
        x = jax.random.normal(k[0], (4, 512, D), jnp.float32)
        centroids = jax.random.normal(k[1], (E, D), jnp.float32) * 0.1
        ln_g = jnp.ones((E, D), jnp.float32)
        ln_b = jnp.zeros((E, D), jnp.float32)
        w1 = jax.random.normal(k[2], (E, F, D), jnp.float32) * (1.0 / np.sqrt(D))
        b1 = jnp.zeros((E, F), jnp.float32)
        w2 = jax.random.normal(k[3], (E, D, F), jnp.float32) * (1.0 / np.sqrt(F))
        b2 = jnp.zeros((E, D), jnp.float32)
        return {'input_features': x, 'centroids': centroids, 'ln_g': ln_g, 'ln_b': ln_b, 'w1': w1, 'b1': b1, 'w2': w2, 'b2': b2}
    _L0_ffn_in = _L0_ffn_setup()

    def _L1_attn_setup():
        import jax, jax.numpy as jnp
        import numpy as np
        B, S, D, H = (2, 512, 256, 16)
        HD = D // H
        MAX_BIAS = 8.0

        def _alibi_bias(T, Sk, dtype):
            slopes = (2.0 ** (-MAX_BIAS / H)) ** jnp.arange(1, H + 1, dtype=dtype)
            qpos = jnp.arange(T)[:, None]
            kpos = jnp.arange(Sk)[None, :]
            rel = -jnp.abs(kpos - qpos).astype(dtype)
            return slopes[:, None, None] * rel[None]
        key = jax.random.key(seed)
        ks = jax.random.split(key, 5)
        sc = 1.0 / np.sqrt(D)
        return {'x': jax.random.normal(ks[0], (B, S, D), jnp.float32), 'Wq': jax.random.normal(ks[1], (D, D), jnp.float32) * sc, 'bq': jnp.zeros((D,), jnp.float32), 'Wk': jax.random.normal(ks[2], (D, D), jnp.float32) * sc, 'bk': jnp.zeros((D,), jnp.float32), 'Wv': jax.random.normal(ks[3], (D, D), jnp.float32) * sc, 'bv': jnp.zeros((D,), jnp.float32), 'Wo': jax.random.normal(ks[4], (D, D), jnp.float32) * sc, 'bo': jnp.zeros((D,), jnp.float32)}
    _L1_attn_in = _L1_attn_setup()

    def _L1_ffn_setup():
        import jax, jax.numpy as jnp
        import numpy as np
        DIM = 256
        HEADS = 8
        NUM_EXPERTS = 16384
        NUM_KEYS = 64
        DIM_KEY = 128
        TOPK = 16

        def _rmsnorm(v, g):
            scale = jnp.sqrt(jnp.asarray(v.shape[-1], v.dtype))
            n = jnp.maximum(jnp.linalg.norm(v, axis=-1, keepdims=True), 1e-12)
            return v / n * g * scale
        key = jax.random.key(seed)
        ks = jax.random.split(key, 6)
        B, N = (2, 128)
        x = jax.random.normal(ks[0], (B, N, DIM), dtype=jnp.float32)
        gamma = jnp.ones((DIM,), dtype=jnp.float32)
        wq = jax.random.normal(ks[1], (2 * HEADS * DIM_KEY, DIM), dtype=jnp.float32) * 0.02
        keys = jax.random.normal(ks[2], (HEADS, NUM_KEYS, 2, DIM_KEY), dtype=jnp.float32) * 0.02
        table_down = jax.random.normal(ks[3], (NUM_EXPERTS, DIM), dtype=jnp.float32) * 0.02
        table_up = jax.random.normal(ks[4], (NUM_EXPERTS, DIM), dtype=jnp.float32) * 0.02
        return {'x': x, 'gamma': gamma, 'wq': wq, 'keys': keys, 'table_down': table_down, 'table_up': table_up}
    _L1_ffn_in = _L1_ffn_setup()
    _d = {'L0_attn_x': _L0_attn_in['x'], 'L0_attn_w_qkv': _L0_attn_in['w_qkv'], 'L0_attn_w_conv1': _L0_attn_in['w_conv1'], 'L0_ffn_centroids': _L0_ffn_in['centroids'], 'L0_ffn_ln_g': _L0_ffn_in['ln_g'], 'L0_ffn_ln_b': _L0_ffn_in['ln_b'], 'L0_ffn_w1': _L0_ffn_in['w1'], 'L0_ffn_b1': _L0_ffn_in['b1'], 'L0_ffn_w2': _L0_ffn_in['w2'], 'L0_ffn_b2': _L0_ffn_in['b2'], 'L1_attn_Wq': _L1_attn_in['Wq'], 'L1_attn_bq': _L1_attn_in['bq'], 'L1_attn_Wk': _L1_attn_in['Wk'], 'L1_attn_bk': _L1_attn_in['bk'], 'L1_attn_Wv': _L1_attn_in['Wv'], 'L1_attn_bv': _L1_attn_in['bv'], 'L1_attn_Wo': _L1_attn_in['Wo'], 'L1_attn_bo': _L1_attn_in['bo'], 'L1_ffn_gamma': _L1_ffn_in['gamma'], 'L1_ffn_wq': _L1_ffn_in['wq'], 'L1_ffn_keys': _L1_ffn_in['keys'], 'L1_ffn_table_down': _L1_ffn_in['table_down'], 'L1_ffn_table_up': _L1_ffn_in['table_up']}
    _x0 = _d['L0_attn_x']
    _d['L0_attn_x'] = jax.random.normal(jax.random.fold_in(jax.random.key(seed), 1), (1, 4096, 256), dtype=_x0.dtype)
    del _x0
    return _d

def reference(L0_attn_x, L0_attn_w_qkv, L0_attn_w_conv1, L0_ffn_centroids, L0_ffn_ln_g, L0_ffn_ln_b, L0_ffn_w1, L0_ffn_b1, L0_ffn_w2, L0_ffn_b2, L1_attn_Wq, L1_attn_bq, L1_attn_Wk, L1_attn_bk, L1_attn_Wv, L1_attn_bv, L1_attn_Wo, L1_attn_bo, L1_ffn_gamma, L1_ffn_wq, L1_ffn_keys, L1_ffn_table_down, L1_ffn_table_up):

    def _L0_attn_ref(x, w_qkv, w_conv1):
        import jax, jax.numpy as jnp
        import numpy as np
        B, N, C = (8, 1024, 256)
        b, n, c = x.shape
        scale = c ** (-0.5)
        qkv = jnp.einsum('bnc,dc->bnd', x, w_qkv)
        q = qkv[..., :c]
        k = qkv[..., c:2 * c]
        v = qkv[..., 2 * c:]
        agent = jnp.einsum('bnc,c->bn', q, w_conv1)
        agent_attn = jax.nn.softmax(jnp.einsum('bn,bnc->bc', agent * scale, k), axis=-1)
        agent_v = jax.nn.softmax(jnp.einsum('bc,bnc->bn', agent_attn, v), axis=-1)
        agent_v = jnp.einsum('bn,bnc->bc', agent_v, v)
        agent_tok = jax.nn.softmax(agent[:, :, None], axis=-1)
        return agent_tok * agent_v[:, None, :]

    def _L0_ffn_ref(input_features, centroids, ln_g, ln_b, w1, b1, w2, b2):
        import jax, jax.numpy as jnp
        import numpy as np
        E, D, F = (8, 256, 1024)
        LN_EPS = 1e-05
        x = input_features.reshape(-1, D)
        aff = jax.lax.stop_gradient(x) @ centroids.T
        assign = jnp.argmax(aff, axis=1)
        onehot = jax.nn.one_hot(assign, E, dtype=x.dtype)
        mu = jnp.mean(x, axis=-1, keepdims=True)
        var = jnp.mean((x - mu) ** 2, axis=-1, keepdims=True)
        xhat = (x - mu) * jax.lax.rsqrt(var + LN_EPS)
        xn = xhat[None, :, :] * ln_g[:, None, :] + ln_b[:, None, :]
        h = jax.nn.relu(jnp.einsum('etd,efd->etf', xn, w1) + b1[:, None, :])
        y = x[None, :, :] + jnp.einsum('etf,edf->etd', h, w2) + b2[:, None, :]
        alpha = jax.nn.sigmoid(x @ centroids.T)
        a = alpha.T[:, :, None]
        gated = a * y + (1.0 - a) * x[None, :, :]
        out = jnp.einsum('te,etd->td', onehot, gated)
        return out.reshape(input_features.shape)

    def _L1_attn_ref(x, Wq, bq, Wk, bk, Wv, bv, Wo, bo):
        import jax, jax.numpy as jnp
        import numpy as np
        B, S, D, H = (2, 512, 256, 16)
        HD = D // H
        MAX_BIAS = 8.0

        def _alibi_bias(T, Sk, dtype):
            slopes = (2.0 ** (-MAX_BIAS / H)) ** jnp.arange(1, H + 1, dtype=dtype)
            qpos = jnp.arange(T)[:, None]
            kpos = jnp.arange(Sk)[None, :]
            rel = -jnp.abs(kpos - qpos).astype(dtype)
            return slopes[:, None, None] * rel[None]
        Bb, Ss, Dd = x.shape
        q = (x @ Wq + bq).reshape(Bb, Ss, H, HD)
        k = (x @ Wk + bk).reshape(Bb, Ss, H, HD)
        v = (x @ Wv + bv).reshape(Bb, Ss, H, HD)
        scores = jnp.einsum('bthd,bshd->bhts', q, k) / jnp.sqrt(jnp.asarray(HD, x.dtype))
        alibi = _alibi_bias(Ss, Ss, x.dtype)
        causal = jnp.triu(jnp.ones((Ss, Ss), bool), 1)
        scores = scores + alibi[None]
        scores = jnp.where(causal[None, None], -jnp.inf, scores)
        attn = jax.nn.softmax(scores, axis=-1)
        out = jnp.einsum('bhts,bshd->bthd', attn, v).reshape(Bb, Ss, Dd)
        return out @ Wo + bo

    def _L1_ffn_ref(x, gamma, wq, keys, table_down, table_up):
        import jax, jax.numpy as jnp
        import numpy as np
        DIM = 256
        HEADS = 8
        NUM_EXPERTS = 16384
        NUM_KEYS = 64
        DIM_KEY = 128
        TOPK = 16

        def _rmsnorm(v, g):
            scale = jnp.sqrt(jnp.asarray(v.shape[-1], v.dtype))
            n = jnp.maximum(jnp.linalg.norm(v, axis=-1, keepdims=True), 1e-12)
            return v / n * g * scale
        B, N, D = x.shape
        xn = _rmsnorm(x, gamma)
        gate = xn
        q = gate @ wq.T
        q = q.reshape(B, N, 2, HEADS, DIM_KEY).transpose(2, 0, 1, 3, 4)
        sim = jnp.einsum('pbnhd,hkpd->pbnhk', q, keys)
        sx, ix = jax.lax.top_k(sim[0], TOPK)
        sy, iy = jax.lax.top_k(sim[1], TOPK)
        all_scores = (sx[..., :, None] + sy[..., None, :]).reshape(B, N, HEADS, TOPK * TOPK)
        all_indices = (ix[..., :, None] * NUM_KEYS + iy[..., None, :]).reshape(B, N, HEADS, TOPK * TOPK)
        scores, pk = jax.lax.top_k(all_scores, TOPK)
        indices = jnp.take_along_axis(all_indices, pk, axis=-1)
        wd = table_down[indices]
        wu = table_up[indices]
        h = jnp.einsum('bnd,bnhkd->bnhk', xn, wd)
        h = jax.nn.gelu(h, approximate=False) * jax.nn.softmax(scores, axis=-1)
        out = jnp.einsum('bnhk,bnhkd->bnd', h, wu)
        return out
    x = L0_attn_x
    xn = _layernorm(x, axis=-1)
    s = _L0_attn_ref(xn, L0_attn_w_qkv, L0_attn_w_conv1)
    g = _silu(_L0_ffn_ref(xn, L0_ffn_centroids, L0_ffn_ln_g, L0_ffn_ln_b, L0_ffn_w1, L0_ffn_b1, L0_ffn_w2, L0_ffn_b2))
    x = x + s * g
    xn = _layernorm(x, axis=-1)
    s = _L1_attn_ref(xn, L1_attn_Wq, L1_attn_bq, L1_attn_Wk, L1_attn_bk, L1_attn_Wv, L1_attn_bv, L1_attn_Wo, L1_attn_bo)
    g = _silu(_L1_ffn_ref(xn, L1_ffn_gamma, L1_ffn_wq, L1_ffn_keys, L1_ffn_table_down, L1_ffn_table_up))
    x = x + s * g
    return x

_drawn_inputs = setup_inputs


def setup_inputs(seed=0):
    import zlib

    import numpy as np

    out = dict(_drawn_inputs(seed))
    spreads = {'L0_ffn_ln_g': (1.0, 0.2),
     'L0_ffn_ln_b': (0.0, 0.1),
     'L0_ffn_b1': (0.0, 0.1),
     'L0_ffn_b2': (0.0, 0.1),
     'L1_attn_bq': (0.0, 0.8),
     'L1_attn_bk': (0.0, 2.0),
     'L1_attn_bv': (0.0, 0.8),
     'L1_attn_bo': (0.0, 2.0),
     'L1_ffn_gamma': (1.0, 0.6)}
    factors = {'L1_attn_Wq': 8.0,
     'L1_attn_Wk': 8.0,
     'L1_attn_Wv': 8.0,
     'L1_attn_Wo': 8.0,
     'L1_ffn_wq': 8.0,
     'L1_ffn_keys': 8.0,
     'L1_ffn_table_down': 8.0,
     'L1_ffn_table_up': 8.0}
    for name, (base, spread) in spreads.items():
        noise = np.random.default_rng([zlib.crc32(name.encode()), seed]).standard_normal(out[name].shape)
        drawn = base * np.exp(spread * noise) if base else spread * noise
        out[name] = jnp.asarray(drawn.astype(out[name].dtype))
    for name, factor in factors.items():
        out[name] = (out[name] * factor).astype(out[name].dtype)
    return out
```

```python
import numpy as np
import concourse.bass as bass
from concourse import mybir
from contextlib import ExitStack

F32, F16, BF16 = mybir.dt.float32, mybir.dt.float16, mybir.dt.bfloat16
U32, I32 = mybir.dt.uint32, mybir.dt.int32
ALU = mybir.AluOpType
ACT = mybir.ActivationFunctionType
AXX = mybir.AxisListType.X

P = 128
N = 4096
C = 256
NT = N // P
CC = C // P
EPS = 1e-5
E = 8
F = 1024
FC = F // P
ET = NT + E
TABLE = 2 * CC + FC


class Chain:

    def __init__(self, eng, sem):
        self.eng, self.sem, self.n, self.base = eng, sem, 0, 0

    def link(self, ins):
        self.n += 1
        ins.then_inc(self.sem, 1)
        self.eng.wait_ge(self.sem, self.base + self.n)

    def enter(self, i, per_step):
        self.outer, self.per_step = self.n, per_step
        self.base, self.n = i * per_step + self.outer, 0

    def leave(self, steps):
        assert self.n == self.per_step, (self.n, self.per_step)
        self.base, self.n = 0, self.outer + steps * self.per_step


class Memory:

    def __init__(self, nc, sems):
        self.nc, self.sems, self.ctx = nc, sems, ExitStack()

    def sb(self, name, shape, dt=F32):
        return self.ctx.enter_context(self.nc.sbuf_tensor(name, shape, dt))

    def ps(self, name, shape, dt=F32):
        return self.ctx.enter_context(self.nc.psum_tensor(name, shape, dt))

    def sem(self, name):
        return self.sems.enter_context(self.nc.semaphore(name))


def row_statistics(nc, vec, ch, src, stats, mv, given):
    with vec.Fori(0, NT) as i:
        nc.vector.bn_stats(stats[:, bass.ds(i, 1), :], src[:, bass.ds(i, 1), :]).then_inc(ch.sem, 1)
    ch.n += NT
    vec.wait_ge(ch.sem, ch.n)
    for i in range(NT):
        nc.vector.bn_aggr(mv[:, i, :], stats[:, i, :]).then_inc(given, 1)


def apply_statistics(nc, vec, ch, src, dst, mv, rstd):
    with vec.Fori(0, NT) as i:
        nc.vector.tensor_scalar(dst[:, bass.ds(i, 1), :], src[:, bass.ds(i, 1), :],
                                mv[:, bass.ds(i, 1), 0:1], rstd[:, bass.ds(i, 1)],
                                ALU.subtract, ALU.mult).then_inc(ch.sem, 1)
    ch.n += NT
    vec.wait_ge(ch.sem, ch.n)


def transpose_rows(nc, mem, tag, ident, src, dst):
    done = mem.sem(f"{tag}_transposed")
    copied = [mem.sem(f"{tag}_copied_dve"), mem.sem(f"{tag}_copied_act")]
    ps = Memory(nc, mem.sems)
    bank = [ps.ps(f"{tag}_ps{b}", [P, 4 * P]) for b in range(4)]
    groups = [(c, g) for g in range(NT // 4) for c in range(CC)]
    with nc.Block() as block:
        @block.tensor
        def _(pe):
            for k, (c, g) in enumerate(groups):
                if k >= 4:
                    pe.wait_ge(copied[k % 2], (k - 4) // 2 + 1)
                for t in range(4):
                    last = nc.tensor.transpose(bank[k % 4][:, t * P:(t + 1) * P],
                                               src[:, 4 * g + t, c * P:(c + 1) * P], ident[:, :])
                last.then_inc(done, 1)

        def take(eng, copy, half):
            for k, (c, g) in enumerate(groups):
                if k % 2 == half:
                    eng.wait_ge(done, k + 1)
                    copy(dst[:, c, g * 4 * P:(g + 1) * 4 * P], bank[k % 4][:, :]).then_inc(copied[half], 1)

        @block.vector
        def _(vec):
            take(vec, nc.vector.tensor_copy, 0)

        @block.scalar
        def _(act):
            take(act, nc.scalar.copy, 1)
    ps.ctx.close()


def l0_normalise(nc, mem, d, m):
    t = Memory(nc, mem.sems)
    X = t.sb("X", [P, NT, C])
    stats, mv = t.sb("stats", [P, NT, 6]), t.sb("mv", [P, NT, 2])
    sd, rstd = t.sb("sd", [P, NT]), t.sb("rstd", [P, NT])
    x_in, given = mem.sem("x_in"), mem.sem("statistics_given")
    rooted, ones_in = mem.sem("deviation_given"), mem.sem("constants_made")
    chain = mem.sem("l0_norm_chain")
    with nc.Block() as block:
        @block.sync
        def _(sp):
            sp.dma_start(X[:, :, :], d["x"].rearrange("(t p) c -> p t c", p=P)).then_inc(x_in, 16)
            for dst, src in m.l0_loads:
                sp.dma_start(dst, src).then_inc(x_in, 16)
            sp.wait_ge(x_in, 16 * (1 + len(m.l0_loads)))

        @block.gpsimd
        def _(pool):
            nc.gpsimd.memset(m.ident[:, :], 0.0).then_inc(ones_in, 1)
            nc.gpsimd.memset(m.ones[:, :], 1.0).then_inc(ones_in, 1)
            nc.gpsimd.memset(m.upto[:, :], 1.0).then_inc(ones_in, 1)
            nc.gpsimd.memset(m.eps[:, :], EPS).then_inc(ones_in, 1)
            pool.wait_ge(ones_in, 4)
            nc.gpsimd.affine_select(out=m.ident[:, :], in_=m.ident[:, :], compare_op=ALU.not_equal, fill=1.0,
                                    base=0, pattern=[[-1, P]], channel_multiplier=1).then_inc(ones_in, 1)
            nc.gpsimd.affine_select(out=m.upto[:, :], in_=m.upto[:, :], compare_op=ALU.is_ge, fill=0.0,
                                    base=0, pattern=[[1, P]], channel_multiplier=-1).then_inc(ones_in, 1)
            nc.gpsimd.iota(m.expert_no[:, :], [[1, E]], base=0, channel_multiplier=0,
                           allow_small_or_imprecise_dtypes=True).then_inc(ones_in, 1)
            nc.gpsimd.iota(m.tile_start[:, :], [[P, ET]], base=0, channel_multiplier=0,
                           allow_small_or_imprecise_dtypes=True).then_inc(ones_in, 1)

        @block.vector
        def _(vec):
            ch = Chain(vec, chain)
            vec.wait_ge(x_in, 16 * (1 + len(m.l0_loads)))
            for n, (src, dst) in enumerate(((X, m.xn), (m.xn, m.xh))):
                row_statistics(nc, vec, ch, src, stats, mv, given)
                vec.wait_ge(rooted, n + 1)
                ch.link(nc.vector.reciprocal(rstd[:, :], sd[:, :]))
                apply_statistics(nc, vec, ch, src, dst, mv, rstd)

        @block.scalar
        def _(act):
            act.wait_ge(ones_in, 8)
            for n in range(2):
                act.wait_ge(given, NT * (n + 1))
                nc.scalar.activation(sd[:, :], mv[:, :, 1], ACT.Sqrt, bias=m.eps[:, :]).then_inc(rooted, 1)
    t.ctx.close()


def l0_global_attention(nc, mem, d, m):
    t = Memory(nc, mem.sems)
    yz = t.sb("yz", [P, CC])
    row = t.sb("row", [1, C])
    erow = t.sb("erow", [1, C])
    small = t.sb("small", [P, 8])
    prow = t.sb("prow", [1, P])
    acol, ucol = t.sb("acol", [P, CC]), t.sb("ucol", [P, CC])
    e_n, w_n = t.sb("e_n", [P, NT]), t.sb("w_n", [P, NT])
    zwide = t.sb("zwide", [P, CC, P])
    ps_a = t.ps("ps_a", [P, NT, 16])
    ps_b = t.ps("ps_b", [P, 512])
    ps_c = t.ps("ps_c", [P, 512])
    s = mem.sem("pe_to_dve")
    v = mem.sem("dve_to_pe")
    a_in, a_out = mem.sem("exp_in_ready"), mem.sem("exp_done")
    chain = mem.sem("l0_attn_chain")
    wq, wk, wv = (slice(i * C, (i + 1) * C) for i in range(3))
    with nc.Block() as block:
        @block.tensor
        def _(pe):
            mm = nc.tensor.matmul
            for c in range(CC):
                for k in range(CC):
                    last = mm(ps_b[:, c:c + 1], m.wqkv[:, k, c * P:(c + 1) * P], m.wconv[:, k:k + 1],
                              start=(k == 0), stop=(k == CC - 1))
            last.then_inc(s, 1)
            pe.wait_ge(v, 1)
            for i in range(NT):
                for c in range(CC):
                    last = mm(ps_a[:, i, 0:E + 1], m.xnT[:, c, i * P:(i + 1) * P], m.affw[:, c, 0:E + 1],
                              start=(c == 0), stop=(c == CC - 1))
            last.then_inc(s, 1)
            pe.wait_ge(v, 2)
            for c in range(CC):
                for i in range(NT):
                    last = mm(ps_b[:, c:c + 1], m.xn[:, i, c * P:(c + 1) * P], m.aff[:, i, E:E + 1],
                              start=(i == 0), stop=(i == NT - 1))
            last.then_inc(s, 1)
            pe.wait_ge(v, 3)
            for c in range(CC):
                last = mm(ps_c[0:1, 0:C], yz[:, c:c + 1], m.wqkvT[:, c, wk], start=(c == 0), stop=(c == CC - 1))
            last.then_inc(s, 1)
            pe.wait_ge(v, 4)
            for k in range(CC):
                last = mm(ps_b[:, k:k + 1], row[0:1, k * P:(k + 1) * P], m.ones[0:1, 0:1], start=True, stop=True)
            last.then_inc(s, 1)
            pe.wait_ge(v, 5)
            for c in range(CC):
                for k in range(CC):
                    last = mm(ps_b[:, c:c + 1], m.wqkv[:, 2 * CC + k, c * P:(c + 1) * P], acol[:, k:k + 1],
                              start=(k == 0), stop=(k == CC - 1))
            last.then_inc(s, 1)
            pe.wait_ge(v, 6)
            for i in range(NT):
                for c in range(CC):
                    last = mm(ps_a[:, i, 0:1], m.xnT[:, c, i * P:(i + 1) * P], ucol[:, c:c + 1],
                              start=(c == 0), stop=(c == CC - 1))
            last.then_inc(s, 1)
            pe.wait_ge(v, 7)
            nc.tensor.transpose(ps_b[0:1, 0:P], small[:, 0:1], m.ident[:, :]).then_inc(s, 1)
            pe.wait_ge(v, 8)
            mm(ps_c[:, 0:1], m.ones[0:1, :], small[0:1, 2:3], start=True, stop=True).then_inc(s, 1)
            pe.wait_ge(a_out, 3)
            mm(ps_b[:, 0:1], m.ones[:, :], small[:, 4:5], start=True, stop=True).then_inc(s, 1)
            pe.wait_ge(v, 9)
            for c in range(CC):
                for i in range(NT):
                    last = mm(ps_c[:, c:c + 1], m.xn[:, i, c * P:(c + 1) * P], w_n[:, i:i + 1],
                              start=(i == 0), stop=(i == NT - 1))
            last.then_inc(s, 1)
            pe.wait_ge(v, 10)
            for c in range(CC):
                last = mm(ps_b[:, 0:C], zwide[:, c, :], m.wqkvT[:, c, wv], start=(c == 0), stop=(c == CC - 1))
            last.then_inc(s, 1)

        @block.vector
        def _(vec):
            ch = Chain(vec, chain)
            vec.wait_ge(s, 1)
            nc.vector.tensor_copy(m.affw[:, :, E], ps_b[:, 0:CC]).then_inc(v, 1)
            vec.wait_ge(s, 2)
            ch.link(nc.vector.tensor_copy(m.aff[:, :, 0:E + 1], ps_a[:, :, 0:E + 1]))
            nc.vector.tensor_tensor(m.tok[:, :], m.aff[:, :, E], m.aff[:, :, E], ALU.subtract).then_inc(v, 1)
            vec.wait_ge(s, 3)
            nc.vector.tensor_scalar(yz[:, :], ps_b[:, 0:CC], float(C) ** -0.5, None, ALU.mult).then_inc(v, 1)
            vec.wait_ge(s, 4)
            nc.vector.tensor_reduce(small[0:1, 5:6], ps_c[0:1, 0:C], AXX, ALU.max, negate=True).then_inc(a_in, 1)
            vec.wait_ge(a_out, 2)
            ch.link(nc.vector.reciprocal(small[0:1, 7:8], small[0:1, 6:7]))
            nc.vector.tensor_scalar(row[0:1, :], erow[0:1, :], small[0:1, 7:8], None, ALU.mult).then_inc(v, 1)
            vec.wait_ge(s, 5)
            nc.vector.tensor_copy(acol[:, :], ps_b[:, 0:CC]).then_inc(v, 1)
            vec.wait_ge(s, 6)
            nc.vector.tensor_copy(ucol[:, :], ps_b[:, 0:CC]).then_inc(v, 1)
            vec.wait_ge(s, 7)
            ch.link(nc.vector.tensor_reduce(small[:, 0:1], ps_a[:, :, 0], AXX, ALU.max))
            nc.vector.tensor_copy(e_n[:, :], ps_a[:, :, 0]).then_inc(v, 1)
            vec.wait_ge(s, 8)
            nc.vector.tensor_reduce(small[0:1, 2:3], ps_b[0:1, 0:P], AXX, ALU.max, negate=True).then_inc(v, 1)
            vec.wait_ge(s, 9)
            nc.vector.tensor_copy(small[:, 3:4], ps_c[:, 0:1]).then_inc(a_in, 1)
            vec.wait_ge(s, 10)
            ch.link(nc.vector.reciprocal(small[:, 1:2], ps_b[:, 0:1]))
            nc.vector.tensor_scalar(w_n[:, :], e_n[:, :], small[:, 1:2], None, ALU.mult).then_inc(v, 1)
            vec.wait_ge(s, 11)
            nc.vector.tensor_copy(zwide[:, :, :], ps_c[:, 0:CC].unsqueeze(2).broadcast_to([P, CC, P])).then_inc(v, 1)
            ch.link(nc.vector.reciprocal(m.sig[:, :], m.tok[:, :]))
            ch.link(nc.vector.tensor_tensor(m.tok[:, :], m.tok[:, :], m.sig[:, :], ALU.mult))
            vec.wait_ge(s, 12)
            ch.link(nc.vector.tensor_copy(m.agv[:, :], ps_b[:, 0:C]))

        @block.scalar
        def _(act):
            act.wait_ge(v, 2)
            nc.scalar.activation(m.tok[:, :], m.tok[:, :], ACT.Exp).then_inc(a_out, 1)
            act.wait_ge(a_in, 1)
            nc.scalar.activation(erow[0:1, :], ps_c[0:1, 0:C], ACT.Exp, bias=small[0:1, 5:6],
                                 accum_out=small[0:1, 6:7]).then_inc(a_out, 1)
            act.wait_ge(a_in, 2)
            nc.scalar.activation(e_n[:, :], e_n[:, :], ACT.Exp, bias=small[:, 3:4],
                                 accum_out=small[:, 4:5]).then_inc(a_out, 1)
    t.ctx.close()


def l0_route(nc, mem, d, m):
    t = Memory(nc, mem.sems)
    top, arg = t.sb("top", [P, NT, 8]), t.sb("arg", [P, NT, 8], U32)
    argf = t.sb("argf", [P, NT])
    hot = t.sb("hot", [P, NT, E])
    rank = t.sb("rank", [P, NT, E])
    tot = t.sb("tot", [P, E, NT + 1])
    scan = t.sb("scan", [P, E, NT + 1])
    zero = t.sb("zero", [P, E, NT + 1])
    cnt, cnti = t.sb("cnt", [P, E]), t.sb("cnti", [P, E], I32)
    posf = t.sb("posf", [P, NT])
    blank = t.sb("blank", [P, C * 8])
    tile_e = t.sb("tile_e", [1, ET])
    ps = t.ps("ps_route", [P, 2, 512])
    hot_given, summed = mem.sem("one_hot_given"), mem.sem("prefix_summed")
    placed, blanked, scattered = mem.sem("places_given"), mem.sem("rows_blanked"), mem.sem("rows_scattered")
    zeroed, sig_in, sig_out = mem.sem("zeroed"), mem.sem("sigmoid_in"), mem.sem("sigmoid_out")
    chain = mem.sem("route_chain")
    with nc.Block() as block:
        @block.vector
        def _(vec):
            ch = Chain(vec, chain)
            ch.link(nc.vector.memset(blank[:, :], 0.0))
            nc.vector.memset(zero[:, :, :], 0.0).then_inc(zeroed, 1)
            for i in range(NT):
                last = nc.vector.max(out=top[:, i, :], in_=m.aff[:, i, 0:E])
            ch.link(last)
            nc.vector.tensor_copy(m.sig[:, :], top[:, :, 0]).then_inc(sig_in, 1)
            for i in range(NT):
                last = nc.vector.max_index(out=arg[:, i, :], in_max=top[:, i, :], in_values=m.aff[:, i, 0:E])
            ch.link(last)
            ch.link(nc.vector.tensor_copy(argf[:, :], arg[:, :, 0]))
            ch.link(nc.vector.tensor_tensor(hot[:, :, :], argf[:, :].unsqueeze(2).broadcast_to([P, NT, E]),
                                            m.expert_no[:, :].unsqueeze(1).broadcast_to([P, NT, E]), ALU.is_equal))
            vec.sem_inc(hot_given, 1)
            vec.wait_ge(summed, 1)
            ch.link(nc.vector.tensor_copy(tot[:, :, 0:NT], ps[:, 1, 0:NT * E].rearrange("p (t e) -> p e t", e=E)))
            ch.link(nc.vector.tensor_copy(rank[:, :, :], ps[:, 0, 0:NT * E].rearrange("p (t e) -> p t e", e=E)))
            ch.link(nc.vector.tensor_reduce(cnt[:, :], tot[:, :, 0:NT], AXX, ALU.add))
            ch.link(nc.vector.tensor_scalar(cnti[:, :], cnt[:, :], float(P - 1), None, ALU.add))
            ch.link(nc.vector.tensor_scalar(cnti[:, :], cnti[:, :], 7, 7, ALU.logical_shift_right,
                                            ALU.logical_shift_left))
            ch.link(nc.vector.tensor_copy(tot[:, :, NT], cnti[:, :]))
            ch.link(nc.vector.tensor_tensor(tot[:, :, NT], tot[:, :, NT], cnt[:, :], ALU.subtract))
            flat = lambda a: a[:, :, :].rearrange("p e t -> p (e t)")
            ch.link(nc.vector.tensor_tensor_scan(flat(scan), flat(tot), flat(zero), 0.0, ALU.add, ALU.add))
            ch.link(nc.vector.memset(tile_e[0:1, :], 0.0))
            for e in range(E - 1):
                ch.link(nc.vector.scalar_tensor_tensor(tile_e[0:1, :], m.tile_start[0:1, :],
                                                       scan[0:1, e, NT:NT + 1], tile_e[0:1, :],
                                                       ALU.is_ge, ALU.add))
            ch.link(nc.vector.tensor_copy(m.tile_expert[0:1, :], tile_e[0:1, :]))
            ch.link(nc.vector.tensor_tensor(scan[:, :, :], scan[:, :, :], tot[:, :, :], ALU.subtract))
            ch.link(nc.vector.tensor_tensor(rank[:, :, :], rank[:, :, :],
                                            scan[:, :, 0:NT].rearrange("p e t -> p t e"), ALU.add))
            ch.link(nc.vector.tensor_tensor(rank[:, :, :], rank[:, :, :], hot[:, :, :], ALU.mult))
            ch.link(nc.vector.tensor_reduce(posf[:, :], rank[:, :, :], AXX, ALU.add))
            ch.link(nc.vector.tensor_scalar(m.place[:, :], posf[:, :], -1.0, None, ALU.add))
            vec.sem_inc(placed, 1)
            vec.wait_ge(sig_out, 1)
            ch.link(nc.vector.tensor_scalar(m.sig[:, :], m.sig[:, :], 1.0, None, ALU.add))
            ch.link(nc.vector.reciprocal(m.sig[:, :], m.sig[:, :]))

        @block.scalar
        def _(act):
            act.wait_ge(sig_in, 1)
            nc.scalar.activation(m.sig[:, :], m.sig[:, :], ACT.Exp, scale=-1.0).then_inc(sig_out, 1)

        @block.tensor
        def _(pe):
            pe.wait_ge(hot_given, 1)
            flat = hot[:, :, :].rearrange("p t e -> p (t e)")
            nc.tensor.matmul(ps[:, 0, 0:NT * E], m.upto[:, :], flat, start=True, stop=True)
            nc.tensor.matmul(ps[:, 1, 0:NT * E], m.ones[:, :], flat, start=True, stop=True).then_inc(summed, 1)

        @block.sync
        def _(sp):
            sp.wait_ge(zeroed, 1)
            for k in range(ET // 8):
                sp.dma_start(d["sorted_x"][k * 8 * P:(k + 1) * 8 * P, :].rearrange("(p r) c -> p (r c)", p=P),
                             blank[:, :]).then_inc(blanked, 16)
            sp.wait_ge(blanked, 16 * (ET // 8))

        @block.gpsimd
        def _(pool):
            pool.wait_ge(placed, 1)
            pool.wait_ge(blanked, 16 * (ET // 8))
            for i in range(NT):
                nc.gpsimd.indirect_dma_start(
                    out=d["sorted_x"], out_offset=bass.IndirectOffsetOnAxis(ap=m.place[:, i:i + 1], axis=0),
                    in_=m.xh[:, i, :], in_offset=None).then_inc(scattered, 16)
            pool.wait_ge(scattered, 16 * NT)
    t.ctx.close()


def l0_experts(nc, mem, d, m):
    t = Memory(nc, mem.sems)
    B = 2
    xs = [t.sb(f"xs{b}", [P, C]) for b in range(B)]
    w1 = [t.sb(f"w1{b}", [P, CC, F]) for b in range(B)]
    w2 = [t.sb(f"w2{b}", [P, FC, C]) for b in range(B)]
    tab = [t.sb(f"tab{b}", [P, TABLE]) for b in range(B)]
    b2 = [t.sb(f"b2{b}", [1, C]) for b in range(B)]
    xe = [t.sb(f"xe{b}", [P, CC, P]) for b in range(B)]
    h = [t.sb(f"h{b}", [P, FC, P]) for b in range(B)]
    y = [t.sb(f"y{b}", [P, C]) for b in range(B)]
    ps_t = [t.ps(f"ps_t{b}", [P, 512]) for b in range(B)]
    ps_h = [t.ps(f"ps_h{b}", [P, 2, 4 * P]) for b in range(B)]
    ps_y = t.ps("ps_y", [P, B, C])
    sem = lambda s: [mem.sem(f"{s}{b}") for b in range(B)]
    loaded = sem("expert_loaded")
    turned, shifted = sem("tile_transposed"), sem("tile_shifted")
    up, relu_v, relu_a = sem("hidden_summed"), sem("relu_dve"), sem("relu_act")
    down, copied, stored = sem("output_summed"), sem("output_copied"), sem("output_stored")
    LOADS = 5
    steps = ET // B
    with nc.Block() as block:
        @block.sync
        def _(sp):
            with sp.Fori(0, steps) as i:
                for b in range(B):
                    j = i * B + b
                    sp.wait_ge(down[b], i + 1)
                    e = sp.value_load(m.tile_expert[0:1, bass.ds(j, 1)], min_val=0, max_val=E - 1)
                    sp.dma_start(xs[b][:, :], d["sorted_x"][bass.ds(j * P, P), :]).then_inc(loaded[b], 16)
                    sp.dma_start(tab[b][:, :], d["table"][bass.ds(e, 1), :, :]).then_inc(loaded[b], 16)
                    sp.dma_start(b2[b][:, :], d["b2"][bass.ds(e, 1), :]).then_inc(loaded[b], 16)
                    sp.dma_start(w1[b][:, :, :], d["w1"][bass.ds(e, 1), :, :, :]).then_inc(loaded[b], 16)
                    sp.dma_start(w2[b][:, :, :], d["w2"][bass.ds(e, 1), :, :, :]).then_inc(loaded[b], 16)

        @block.tensor
        def _(pe):
            mm = nc.tensor.matmul
            for b in range(B):
                pe.sem_inc(down[b], 1)
            with pe.Fori(0, steps) as i:
                for b in range(B):
                    pe.wait_ge(loaded[b], (i + 1) * 16 * LOADS)
                    for c in range(CC):
                        last = nc.tensor.transpose(ps_t[b][:, c * P:(c + 1) * P], xs[b][:, c * P:(c + 1) * P],
                                                   m.ident[:, :])
                    last.then_inc(turned[b], 1)
                    pe.wait_ge(shifted[b], i + 1)
                    for f in range(FC):
                        for c in range(CC):
                            last = mm(ps_h[b][:, f // 4, (f % 4) * P:(f % 4 + 1) * P],
                                      w1[b][:, c, f * P:(f + 1) * P], xe[b][:, c, :],
                                      start=(c == 0), stop=(c == CC - 1))
                        if f % 4 == 3:
                            last.then_inc(up[b], 1)
                    pe.wait_ge(copied[b], i + 1)
                    mm(ps_y[:, b, :], m.ones[0:1, :], b2[b][0:1, :], start=True, stop=False)
                    pe.wait_ge(relu_v[b], i + 1)
                    for f in range(FC):
                        if f == 4:
                            pe.wait_ge(relu_a[b], i + 1)
                        last = mm(ps_y[:, b, :], h[b][:, f, :], w2[b][:, f, :], start=False, stop=(f == FC - 1))
                    last.then_inc(down[b], 1)

        @block.vector
        def _(vec):
            for b in range(B):
                vec.sem_inc(copied[b], 1)
            with vec.Fori(0, steps) as i:
                for b in range(B):
                    vec.wait_ge(turned[b], i + 1)
                    for c in range(CC):
                        last = nc.vector.tensor_scalar(xe[b][:, c, :], ps_t[b][:, c * P:(c + 1) * P],
                                                       tab[b][:, c:c + 1], tab[b][:, CC + c:CC + c + 1],
                                                       ALU.mult, ALU.add)
                    last.then_inc(shifted[b], 1)
                    vec.wait_ge(up[b], 2 * i + 1)
                    for f in range(4):
                        last = nc.vector.tensor_scalar(h[b][:, f, :], ps_h[b][:, 0, f * P:(f + 1) * P],
                                                       tab[b][:, 2 * CC + f:2 * CC + f + 1], 0.0, ALU.add, ALU.max)
                    last.then_inc(relu_v[b], 1)
                    vec.wait_ge(down[b], i + 2)
                    vec.wait_ge(stored[b], 16 * (i + 1))
                    nc.vector.tensor_copy(y[b][:, :], ps_y[:, b, :]).then_inc(copied[b], 1)

        @block.scalar
        def _(act):
            for b in range(B):
                act.sem_inc(stored[b], 16)
            with act.Fori(0, steps) as i:
                for b in range(B):
                    act.wait_ge(up[b], 2 * i + 2)
                    for f in range(4, FC):
                        last = nc.scalar.activation(h[b][:, f, :], ps_h[b][:, 1, (f - 4) * P:(f - 3) * P], ACT.Relu,
                                                    bias=tab[b][:, 2 * CC + f:2 * CC + f + 1])
                    last.then_inc(relu_a[b], 1)
                    act.wait_ge(copied[b], i + 2)
                    act.dma_start(d["sorted_y"][bass.ds((i * B + b) * P, P), :], y[b][:, :]).then_inc(stored[b], 16)
            for b in range(B):
                act.wait_ge(stored[b], 16 * (steps + 1))
    t.ctx.close()


def l0_combine(nc, mem, d, m):
    t = Memory(nc, mem.sems)
    H = NT // 2
    got = t.sb("got", [P, H, C])
    X = t.sb("Xr", [P, H, C])
    y_in, x_in = mem.sem("y_gathered"), mem.sem("x_again")
    given, gated, out = mem.sem("silu_in"), mem.sem("silu_out"), mem.sem("x1_made")
    stored = mem.sem("x1_stored")
    chain = mem.sem("combine_chain")
    x_t = d["x"].rearrange("(t p) c -> p t c", p=P)
    x1_t = d["x1"].rearrange("(t p) c -> p t c", p=P)
    with nc.Block() as block:
        @block.gpsimd
        def _(pool):
            for k in range(2):
                if k:
                    pool.wait_ge(out, 1)
                    pool.wait_ge(stored, 16)
                for i in range(H):
                    nc.gpsimd.indirect_dma_start(
                        out=got[:, i, :], out_offset=None, in_=d["sorted_y"],
                        in_offset=bass.IndirectOffsetOnAxis(ap=m.place[:, k * H + i:k * H + i + 1], axis=0)
                    ).then_inc(y_in, 16)

        @block.sync
        def _(sp):
            for k in range(2):
                if k:
                    sp.wait_ge(stored, 16)
                sp.dma_start(X[:, :, :], x_t[:, k * H:(k + 1) * H, :]).then_inc(x_in, 16)
                sp.wait_ge(out, k + 1)
                sp.dma_start(x1_t[:, k * H:(k + 1) * H, :], X[:, :, :]).then_inc(stored, 16)
            sp.wait_ge(stored, 32)

        @block.vector
        def _(vec):
            ch = Chain(vec, chain)
            for k in range(2):
                vec.wait_ge(y_in, 16 * H * (k + 1))
                for i in range(H):
                    g = k * H + i
                    last = nc.vector.scalar_tensor_tensor(got[:, i, :], got[:, i, :], m.sig[:, g:g + 1],
                                                          m.xn[:, g, :], ALU.mult, ALU.add)
                last.then_inc(given, 1)
                vec.wait_ge(gated, k + 1)
                for i in range(H):
                    g = k * H + i
                    last = nc.vector.scalar_tensor_tensor(got[:, i, :], m.agv[:, :], m.tok[:, g:g + 1],
                                                          got[:, i, :], ALU.mult, ALU.mult)
                ch.link(last)
                vec.wait_ge(x_in, 16 * (k + 1))
                nc.vector.tensor_tensor(X[:, :, :], X[:, :, :], got[:, :, :], ALU.add).then_inc(out, 1)

        @block.scalar
        def _(act):
            for k in range(2):
                act.wait_ge(given, k + 1)
                nc.scalar.activation(got[:, :, :], got[:, :, :], ACT.Silu).then_inc(gated, 1)
    t.ctx.close()


H = 16
HD = C // H
PAIRS = H // 2
QB = 512
NQ = N // QB
QT = QB // P
GK = 2
ROWS = 64
SPEC = 32
NSPEC = 6
LO = SPEC + NSPEC
MASKED = -1e30
MSCALE = 256.0
GROUPS = sum(GK * (q + 1) for q in range(NQ))
CHUNKS = sum(QT * (q + 1) for q in range(NQ))


class Count:

    def __init__(self, mem, name, per, credit=0):
        self.sem, self.per, self.credit = mem.sem(name), per, credit

    def at(self, i, k):
        return i * self.per + (self.credit + k)


def l1_normalise(nc, mem, d, m):
    t = Memory(nc, mem.sems)
    X = t.sb("X1", [P, NT, C])
    stats, mv = t.sb("stats1", [P, NT, 6]), t.sb("mv1", [P, NT, 2])
    sd, rstd, sq = t.sb("sd1", [P, NT]), t.sb("rstd1", [P, NT]), t.sb("sq1", [P, NT])
    x_in, given, rooted = mem.sem("x1_in"), mem.sem("stats1_given"), mem.sem("dev1_given")
    chain = mem.sem("l1_norm_chain")
    with nc.Block() as block:
        @block.sync
        def _(sp):
            sp.dma_start(X[:, :, :], d["x1"].rearrange("(t p) c -> p t c", p=P)).then_inc(x_in, 16)

        @block.vector
        def _(vec):
            ch = Chain(vec, chain)
            vec.wait_ge(x_in, 16)
            row_statistics(nc, vec, ch, X, stats, mv, given)
            vec.wait_ge(rooted, 1)
            ch.link(nc.vector.reciprocal(rstd[:, :], sd[:, :]))
            apply_statistics(nc, vec, ch, X, m.xn, mv, rstd)
            row_statistics(nc, vec, ch, m.xn, stats, mv, given)
            vec.wait_ge(given, 2 * NT)
            ch.link(nc.vector.tensor_tensor(sq[:, :], mv[:, :, 0], mv[:, :, 0], ALU.mult))
            nc.vector.tensor_tensor(sq[:, :], sq[:, :], mv[:, :, 1], ALU.add).then_inc(given, 1)
            vec.wait_ge(rooted, 2)
            ch.link(nc.vector.tensor_scalar(sd[:, :], sd[:, :], 1e-12, None, ALU.max))
            ch.link(nc.vector.reciprocal(rstd[:, :], sd[:, :]))
            with vec.Fori(0, NT) as i:
                nc.vector.tensor_scalar(m.xg[:, bass.ds(i, 1), :], m.xn[:, bass.ds(i, 1), :],
                                        rstd[:, bass.ds(i, 1)], float(C) ** 0.5, ALU.mult, ALU.mult
                                        ).then_inc(ch.sem, 1)
            ch.n += NT
            vec.wait_ge(ch.sem, ch.n)

        @block.scalar
        def _(act):
            act.wait_ge(given, NT)
            nc.scalar.activation(sd[:, :], mv[:, :, 1], ACT.Sqrt, bias=m.eps[:, :]).then_inc(rooted, 1)
            act.wait_ge(given, 2 * NT + 1)
            nc.scalar.activation(sd[:, :], sq[:, :], ACT.Sqrt, scale=float(C)).then_inc(rooted, 1)
    t.ctx.close()


def l1_gain(nc, mem, d, m, xgT):
    gamma = m.gamma
    g_in, scaled, kept = mem.sem("gamma_in"), mem.sem("gamma_applied"), mem.sem("xg_kept")
    with nc.Block() as block:
        @block.sync
        def _(sp):
            sp.dma_start(gamma[:, :], d["gamma"]).then_inc(g_in, 16)
            for c in range(CC):
                sp.wait_ge(scaled, c + 1)
                sp.dma_start(d["xgT"][:, c, :], xgT[:, c, :]).then_inc(kept, 16)
            sp.wait_ge(kept, 16 * CC)

        @block.vector
        def _(vec):
            vec.wait_ge(g_in, 16)
            for c in range(CC):
                nc.vector.tensor_scalar(xgT[:, c, :], xgT[:, c, :], gamma[:, c:c + 1], None,
                                        ALU.mult).then_inc(scaled, 1)


def l1_values(nc, mem, d, m):
    t = Memory(nc, mem.sems)
    wv, bv = t.sb("wv", [P, CC, C]), t.sb("bv", [P, C])
    ps = [t.ps(f"ps_v{b}", [P, 2, C]) for b in range(4)]
    w_in, summed, added = mem.sem("wv_in"), mem.sem("v_summed"), mem.sem("v_added")
    with nc.Block() as block:
        @block.sync
        def _(sp):
            sp.dma_start(wv[:, :, :], d["wv"].rearrange("(k p) c -> p k c", p=P)).then_inc(w_in, 16)
            sp.dma_start(bv[:, :], d["bv"].broadcast_to([P, C])).then_inc(w_in, 16)
            for dst, src in m.attn_loads:
                sp.dma_start(dst, src).then_inc(w_in, 16)
            sp.wait_ge(w_in, 16 * (2 + len(m.attn_loads)))

        @block.gpsimd
        def _(pool):
            for k, (part, value) in enumerate([(m.vall[:, :, :, HD:HD + 1], 1.0), (m.vpair[:, :, :, HD:], 0.0),
                                               (m.qa[0][ROWS:P, :], 0.0), (m.qa[1][0:ROWS, :], 0.0),
                                               (m.stage[:, :, :], 0.0), (m.identb[:, :], 0.0),
                                               (m.after[:, :], 0.0), (m.before[:, :], 0.0)]):
                nc.gpsimd.memset(part, value).then_inc(added, 1)
                pool.wait_ge(added, k + 1)
            for mask, op, fill, base, step in ((m.identb, ALU.not_equal, 1.0, 0, -1), (m.after, ALU.is_ge, MASKED, 0, -1),
                                               (m.before, ALU.is_ge, MASKED, P - QB, 1)):
                nc.gpsimd.affine_select(out=mask[:, :], in_=mask[:, :], compare_op=op, fill=fill, base=base,
                                        pattern=[[step, mask.shape[1]]], channel_multiplier=-step).then_inc(added, 1)

        @block.tensor
        def _(pe):
            pe.wait_ge(w_in, 16 * (2 + len(m.attn_loads)))
            for g in range(NT // 2):
                if g >= 4:
                    pe.wait_ge(m.v_free, g - 3)
                for j in range(2):
                    i = 2 * g + j
                    for c in range(CC):
                        last = nc.tensor.matmul(ps[g % 4][:, j, :], m.xnT[:, c, i * P:(i + 1) * P], wv[:, c, :],
                                                start=(c == 0), stop=(c == CC - 1))
                last.then_inc(summed, 1)

        @block.vector
        def _(vec):
            vec.wait_ge(w_in, 16 * (2 + len(m.attn_loads)))
            for g in range(NT // 2):
                vec.wait_ge(summed, g + 1)
                nc.vector.tensor_tensor(
                    m.vall[:, 2 * g:2 * g + 2, :, 0:HD],
                    ps[g % 4][:, :, :].rearrange("p j (h e) -> p j h e", h=H),
                    bv[:, :].rearrange("p (h e) -> p h e", h=H).unsqueeze(1).broadcast_to([P, 2, H, HD]),
                    ALU.add).then_inc(m.v_free, 1)
    t.ctx.close()


def l1_attention(nc, mem, d, m):
    t = Memory(nc, mem.sems)
    wqk = t.sb("wqk", [P, 2, CC, P])
    x32 = [t.sb(f"x32_{b}", [P, QB]) for b in range(2)]
    h16 = [t.sb(f"h16_{b}", [P, QB], F16) for b in range(2)]
    pT = [t.sb(f"pT{b}", [P, GK, QB]) for b in range(4)]
    o_sb = t.sb("o_sb", [P, QB])
    mxc = t.sb("mxc", [P, 2, QT, NQ])
    mx, mlow = t.sb("mx", [P, 2, QT]), t.sb("mlow", [P, 2, QT], F16)
    rden = t.sb("rden", [P, QT, 2])
    abias = t.sb("abias_pair", [P, 2, GK * NQ])
    gates = mem.sem("attention_gates")
    st = t.ps("st", [P, 2, GK, QB])
    sq = t.ps("sq", [P, 2, QB])
    o4 = t.ps("o4", [P, QB])
    misc = t.ps("misc", [P, 512])
    turned = misc[:, 0:256].bitcast(F16).rearrange("p (a q) -> p a q", a=QT)
    picked = misc[:, 256:256 + QT * 2 * (HD + 1)].rearrange("p (a h e) -> p a h e", a=QT, h=2)
    ka, qa = m.ka, m.qa
    NCH = 2 * NQ
    c_w = Count(mem, "pair_weights_in", 16)
    c_proj = Count(mem, "projected", NCH)
    c_x32 = Count(mem, "projection_copied", NCH, 4)
    c_h16 = Count(mem, "high_halves", NCH)
    c_part = Count(mem, "halves_split", NCH, 2)
    c_spec = Count(mem, "special_rows_in", 64)
    c_vp = Count(mem, "pair_values_copied", 1)
    c_gs = Count(mem, "slopes_staged", 2)
    c_sq = Count(mem, "scores_for_maxima", 2 * CHUNKS)
    c_max = Count(mem, "maxima_taken", 2 * CHUNKS, 2)
    c_stage = Count(mem, "maxima_staged", NQ)
    c_turn = Count(mem, "maxima_transposed", NQ)
    c_rows = Count(mem, "maxima_rows_in", NQ)
    c_st = Count(mem, "scores_ready", 2 * GROUPS)
    c_exp = Count(mem, "exponentials_ready", 2 * GROUPS, 2)
    c_pv = Count(mem, "exponentials_used", GROUPS, 2)
    c_osb = Count(mem, "block_copied", NQ, 1)
    c_pick = Count(mem, "block_picked", NQ)
    c_att = Count(mem, "block_normalised", NQ, 1)
    chain = mem.sem("attention_chain")

    def sq_items(b):
        return [(hd, a, k) for hd in range(2) for a in range(QT) for k in range(b + 1)]

    def sq_base(b):
        return sum(2 * QT * (x + 1) for x in range(b))

    def g_base(b):
        return sum(GK * (x + 1) for x in range(b))

    with nc.Block() as block:
        @block.sync
        def _(sp):
            with sp.Fori(0, PAIRS) as i:
                sp.wait_ge(c_part.sem, c_part.at(i, 0))
                sp.dma_start(wqk[:, :, :, :], d["wqk"][bass.ds(i, 1), :, :, :, :]).then_inc(c_w.sem, 16)
                sp.wait_ge(c_part.sem, c_part.at(i, NCH))
                for hd in range(2):
                    r = hd * ROWS + SPEC
                    sp.dma_start(ka[r:r + NSPEC, :], d["kspec"][bass.ds(i, 1), hd, :, :]).then_inc(c_spec.sem, 16)
                    sp.dma_start(qa[hd][r:r + NSPEC, :], d["qspec"]).then_inc(c_spec.sem, 16)

        @block.gpsimd
        def _(pool):
            with pool.Fori(0, PAIRS) as i:
                pool.wait_ge(c_pv.sem, c_pv.at(i, 0))
                pool.sem_inc(gates, 1)
                nc.gpsimd.tensor_copy(m.vpair[:, :, :, 0:HD + 1],
                                      m.vall[:, :, bass.ds(2 * i, 2), :]).then_inc(c_vp.sem, 1)
                for n in range(NCH):
                    pool.wait_ge(c_x32.sem, c_x32.at(i, n + 1))
                    pool.sem_inc(gates, 1)
                    nc.gpsimd.tensor_copy(h16[n % 2][:, :], x32[n % 2][:, :]).then_inc(c_h16.sem, 1)

        @block.scalar
        def _(act):
            act.sem_inc(c_x32.sem, c_x32.credit)
            act.sem_inc(c_exp.sem, c_exp.credit)
            with act.Fori(0, PAIRS) as i:
                for n in range(NCH):
                    act.wait_ge(c_proj.sem, c_proj.at(i, n + 1))
                    act.wait_ge(c_part.sem, c_part.at(i, n - 1))
                    act.sem_inc(gates, 1)
                    which = n // NQ
                    nc.scalar.activation(x32[n % 2][:, :], st[:, (n % 4) // 2, n % 2, :], ACT.Identity,
                                         bias=m.bqk[:, which, bass.ds(i, 1)],
                                         scale=(float(HD) ** -0.5 if which else 1.0)).then_inc(c_x32.sem, 1)
                act.wait_ge(c_gs.sem, c_gs.at(i, 2))
                for b in range(NQ):
                    for g in range(GK * (b + 1)):
                        q0 = QB // 2 if g == GK * b + 1 else 0
                        for hd in range(2):
                            n = 2 * (g_base(b) + g) + hd
                            act.wait_ge(c_st.sem, c_st.at(i, n + 1))
                            act.wait_ge(c_pv.sem, c_pv.at(i, g_base(b) + g - 1))
                            nc.scalar.activation(
                                pT[n % 4][:, :, q0:], st[:, n % 2, :, q0:], ACT.Exp,
                                bias=abias[:, hd, g - GK * b + GK * (NQ - 1):g - GK * b + GK * (NQ - 1) + 1]
                            ).then_inc(c_exp.sem, 1)

        @block.vector
        def _(vec):
            vec.sem_inc(c_part.sem, c_part.credit)
            vec.sem_inc(c_max.sem, c_max.credit)
            vec.sem_inc(c_osb.sem, c_osb.credit)
            vec.sem_inc(c_att.sem, c_att.credit)
            ch = Chain(vec, chain)

            def maxima(i, b, lo, hi):
                items = sq_items(b)
                for x in range(lo, hi):
                    hd, a, k = items[x]
                    n = sq_base(b) + x
                    w = (a + 1) * P if k == b else QB
                    vec.wait_ge(c_sq.sem, c_sq.at(i, n + 1))
                    nc.vector.tensor_reduce(mxc[:, hd, a, k:k + 1], sq[:, n % 2, 0:w], AXX,
                                            ALU.max).then_inc(c_max.sem, 1)

            def stage_maxima(i, b):
                vec.wait_ge(c_max.sem, c_max.at(i, sq_base(b + 1)))
                ch.link(nc.vector.tensor_reduce(mx[:, :, :], mxc[:, :, :, 0:b + 1], AXX, ALU.max))
                for hd in range(2):
                    last = nc.vector.tensor_scalar(mx[:, hd, :], mx[:, hd, :], -1.0 / MSCALE,
                                                   m.start[:, bass.ds(2 * i + hd, 1), b], ALU.mult, ALU.add)
                ch.link(last)
                hi = m.stage[:, :, :].rearrange("p a (h r) -> p h a r", h=2)
                ch.link(nc.vector.tensor_copy(hi[:, :, :, SPEC], mx[:, :, :]))
                nc.vector.tensor_tensor(hi[:, :, :, SPEC + 1], mx[:, :, :], hi[:, :, :, SPEC],
                                        ALU.subtract).then_inc(c_stage.sem, 1)

            def take_rows(i, b):
                vec.wait_ge(c_turn.sem, c_turn.at(i, b + 1))
                for hd in range(2):
                    r = hd * ROWS + SPEC
                    last = nc.vector.tensor_copy(
                        qa[hd][r:r + NSPEC, b * QB:(b + 1) * QB].rearrange("p (a q) -> p a q", a=QT),
                        turned[r:r + NSPEC, :, :])
                last.then_inc(c_rows.sem, 1)

            def finish_block(i, b):
                vec.wait_ge(c_pv.sem, c_pv.at(i, g_base(b + 1)))
                nc.vector.tensor_copy(o_sb[:, :], o4[:, :]).then_inc(c_osb.sem, 1)
                vec.wait_ge(c_pick.sem, c_pick.at(i, b + 1))
                ch.link(nc.vector.reciprocal(rden[:, :, :], picked[:, :, :, HD]))
                nc.vector.tensor_tensor(
                    m.att[:, b * QT:(b + 1) * QT, bass.ds(2 * HD * i, 2 * HD)].rearrange("p a (h e) -> p a h e", h=2),
                    picked[:, :, :, 0:HD], rden[:, :, :].unsqueeze(3).broadcast_to([P, QT, 2, HD]),
                    ALU.mult).then_inc(c_att.sem, 1)

            with vec.Fori(0, PAIRS) as i:
                ch.enter(i, NQ * 4 + 0)
                for n in range(NCH):
                    vec.wait_ge(c_h16.sem, c_h16.at(i, n + 1))
                    c = n % NQ
                    if n < NQ:
                        last = nc.vector.scalar_tensor_tensor(ka[:, c * QB:(c + 1) * QB], h16[n % 2][:, :],
                                                              m.minus_k[:, :], x32[n % 2][:, :],
                                                              ALU.mult, ALU.add)
                    else:
                        for hd in range(2):
                            r = slice(hd * ROWS, (hd + 1) * ROWS)
                            last = nc.vector.scalar_tensor_tensor(qa[hd][r, c * QB:(c + 1) * QB],
                                                                  h16[n % 2][r, :], m.minus_q[r, :],
                                                                  x32[n % 2][r, :], ALU.mult, ALU.add)
                    last.then_inc(c_part.sem, 1)
                for hd in range(2):
                    last = nc.vector.tensor_copy(
                        m.stage[:, :, hd * ROWS + SPEC + 2:hd * ROWS + SPEC + 4],
                        m.slopes[:, bass.ds(2 * i + hd, 1), :].broadcast_to([P, QT, 2]))
                last.then_inc(c_gs.sem, 1)
                nc.vector.tensor_copy(abias[:, :, :], m.abias[:, bass.ds(2 * i, 2), :]).then_inc(c_gs.sem, 1)
                maxima(i, 0, 0, len(sq_items(0)))
                stage_maxima(i, 0)
                take_rows(i, 0)
                for b in range(NQ):
                    if b + 1 < NQ:
                        maxima(i, b + 1, 0, len(sq_items(b + 1)))
                        stage_maxima(i, b + 1)
                        take_rows(i, b + 1)
                    finish_block(i, b)
                ch.leave(PAIRS)

        @block.tensor
        def _(pe):
            mm = nc.tensor.matmul
            pe.sem_inc(c_pv.sem, c_pv.credit)

            def maxima_scores(i, b, lo, hi):
                items = sq_items(b)
                for x in range(lo, hi):
                    hd, a, k = items[x]
                    n = sq_base(b) + x
                    w = (a + 1) * P if k == b else QB
                    pe.wait_ge(c_max.sem, c_max.at(i, n - 1))
                    q = b * QB + a * P
                    last = mm(sq[:, n % 2, 0:w], qa[hd][:, q:q + P], ka[:, k * QB:k * QB + w],
                              start=True, stop=(k < b))
                    if k == b:
                        last = mm(sq[:, n % 2, a * P:w], m.identb[:, :], m.after[:, :], start=False, stop=True)
                    last.then_inc(c_sq.sem, 1)

            def scores(i, b, g, hd):
                n = 2 * (g_base(b) + g) + hd
                q0 = QB // 2 if g == GK * b + 1 else 0
                pe.wait_ge(c_exp.sem, c_exp.at(i, n - 1))
                for j in range(GK):
                    kt = GK * g + j
                    r = kt - QT * b
                    last = mm(st[:, n % 2, j, q0:], ka[:, kt * P:(kt + 1) * P],
                              qa[hd][:, b * QB + q0:(b + 1) * QB], start=True, stop=(r < 0))
                    if r >= 0:
                        w = (r + 1) * P - q0
                        last = mm(st[:, n % 2, j, q0:q0 + w], m.identb[:, :], m.before[:, QB - w:],
                                  start=False, stop=True)
                last.then_inc(c_st.sem, 1)

            def weighted(i, b, g):
                q0 = QB // 2 if g == GK * b + 1 else 0
                n = 2 * (g_base(b) + g)
                pe.wait_ge(c_exp.sem, c_exp.at(i, n + 2))
                if g == 0:
                    pe.wait_ge(c_osb.sem, c_osb.at(i, b))
                for hd in range(2):
                    for j in range(GK):
                        r = (GK * hd + j) * 32
                        last = mm(o4[r:r + 32, q0:], m.vpair[:, GK * g + j, hd, :], pT[(n + hd) % 4][:, j, q0:],
                                  start=(g == 0), stop=(g == GK * b + 1))
                last.then_inc(c_pv.sem, 1)

            def turn(i, b):
                pe.wait_ge(c_stage.sem, c_stage.at(i, b + 1))
                for a in range(QT):
                    last = nc.tensor.transpose(turned[:, a, :], m.stage[:, a, :], m.ident16[:, :])
                last.then_inc(c_turn.sem, 1)

            def pick(i, b):
                pe.wait_ge(c_osb.sem, c_osb.at(i, b + 1))
                pe.wait_ge(c_att.sem, c_att.at(i, b))
                for a in range(QT):
                    last = mm(misc[:, 256 + a * 2 * (HD + 1):256 + (a + 1) * 2 * (HD + 1)],
                              o_sb[:, a * P:(a + 1) * P], m.pick[:, :], start=True, stop=True)
                last.then_inc(c_pick.sem, 1)

            with pe.Fori(0, PAIRS) as i:
                pe.wait_ge(c_w.sem, c_w.at(i, 16))
                pe.wait_ge(c_exp.sem, c_exp.at(i, 0))
                for n in range(NCH):
                    c = n % NQ
                    pe.wait_ge(c_x32.sem, c_x32.at(i, n - 3))
                    for k in range(CC):
                        last = mm(st[:, (n % 4) // 2, n % 2, :], wqk[:, n // NQ, k, :],
                                  m.xnT[:, k, c * QB:(c + 1) * QB], start=(k == 0), stop=(k == CC - 1))
                    last.then_inc(c_proj.sem, 1)
                pe.wait_ge(c_x32.sem, c_x32.at(i, NCH))
                pe.wait_ge(c_spec.sem, c_spec.at(i, 64))
                pe.wait_ge(c_vp.sem, c_vp.at(i, 1))
                pe.wait_ge(c_gs.sem, c_gs.at(i, 2))
                maxima_scores(i, 0, 0, len(sq_items(0)))
                turn(i, 0)
                for b in range(NQ):
                    pe.wait_ge(c_rows.sem, c_rows.at(i, b + 1))
                    G = GK * (b + 1)
                    items = len(sq_items(b + 1)) if b + 1 < NQ else 0
                    for g in range(G):
                        for hd in range(2):
                            scores(i, b, g, hd)
                            k = 2 * g + hd
                            if k < 2 * (G - 1):
                                maxima_scores(i, b + 1, items * k // (2 * G - 2), items * (k + 1) // (2 * G - 2)) \
                                    if items else None
                        if g >= 1:
                            weighted(i, b, g - 1)
                    if items:
                        turn(i, b + 1)
                    weighted(i, b, G - 1)
                    pick(i, b)
    t.ctx.close()


def l1_output(nc, mem, d, m, attT):
    t = Memory(nc, mem.sems)
    wo, bo = t.sb("wo", [P, CC, C]), t.sb("bo", [P, C])
    s = [t.sb(f"s_sb{b}", [P, 4, C]) for b in range(2)]
    ps = [t.ps(f"ps_o{b}", [P, 4, C]) for b in range(2)]
    w_in, summed, added = mem.sem("wo_in"), mem.sem("o_summed"), mem.sem("o_added")
    kept = [mem.sem(f"s_kept{b}") for b in range(2)]
    s_t = d["s1"].rearrange("(t p) c -> p t c", p=P)
    with nc.Block() as block:
        @block.sync
        def _(sp):
            sp.dma_start(wo[:, :, :], d["wo"].rearrange("(k p) c -> p k c", p=P)).then_inc(w_in, 16)
            sp.dma_start(bo[:, :], d["bo"].broadcast_to([P, C])).then_inc(w_in, 16)
            for g in range(NT // 4):
                sp.wait_ge(added, g + 1)
                sp.dma_start(s_t[:, 4 * g:4 * g + 4, :], s[g % 2][:, :, :]).then_inc(kept[g % 2], 16)
            for b in range(2):
                sp.wait_ge(kept[b], 16 * (NT // 8))

        @block.tensor
        def _(pe):
            pe.wait_ge(w_in, 32)
            for g in range(NT // 4):
                if g >= 2:
                    pe.wait_ge(added, g - 1)
                for j in range(4):
                    i = 4 * g + j
                    for c in range(CC):
                        last = nc.tensor.matmul(ps[g % 2][:, j, :], attT[:, c, i * P:(i + 1) * P], wo[:, c, :],
                                                start=(c == 0), stop=(c == CC - 1))
                last.then_inc(summed, 1)

        @block.vector
        def _(vec):
            vec.wait_ge(w_in, 32)
            for g in range(NT // 4):
                vec.wait_ge(summed, g + 1)
                if g >= 2:
                    vec.wait_ge(kept[g % 2], 16 * (g // 2))
                nc.vector.tensor_tensor(s[g % 2][:, :, :], ps[g % 2][:, :, :],
                                        bo[:, :].unsqueeze(1).broadcast_to([P, 4, C]), ALU.add).then_inc(added, 1)
    t.ctx.close()


def layer1(nc, mem, sems, d, m):
    a = Memory(nc, sems)
    m.xnT = a.sb("xn1T", [P, CC, N])
    m.gamma = a.sb("gamma", [P, CC])
    b = Memory(nc, sems)
    m.xn, m.xg = b.sb("xn1", [P, NT, C]), b.sb("xg", [P, NT, C])
    l1_normalise(nc, mem, d, m)
    transpose_rows(nc, mem, "xg", m.ident, m.xg, m.xnT)
    l1_gain(nc, mem, d, m, m.xnT)
    transpose_rows(nc, mem, "xn1", m.ident, m.xn, m.xnT)
    b.ctx.close()
    b = Memory(nc, sems)
    m.att = b.sb("att", [P, NT, C])
    c = Memory(nc, sems)
    m.vall = c.sb("vall", [P, NT, H, HD + 1])
    m.vpair = c.sb("vpair", [P, NT, 2, 32])
    m.ka = c.sb("ka", [P, N], F16)
    m.qa = [c.sb(f"qa{h}", [P, N], F16) for h in range(2)]
    m.stage = c.sb("stage", [P, QT, P], F16)
    m.slopes = c.sb("slopes", [P, H, 2], F16)
    m.start = c.sb("start", [P, H, NQ])
    m.abias = c.sb("abias", [P, H, GK * NQ])
    m.bqk = c.sb("bqk", [P, 2, PAIRS])
    m.minus_k, m.minus_q = c.sb("minus_k", [P, 1]), c.sb("minus_q", [P, 1])
    m.ident16, m.identb = c.sb("ident16", [P, P], F16), c.sb("identb", [P, P], BF16)
    m.after, m.before = c.sb("after", [P, P], BF16), c.sb("before", [P, QB], BF16)
    m.pick = c.sb("pick", [P, 2 * (HD + 1)])
    m.v_free = mem.sem("v_bank_free")
    m.attn_loads = [(m.slopes[:, :, :], d["slopes"]), (m.start[:, :, :], d["start"]), (m.abias[:, :, :], d["abias"]),
                    (m.bqk[:, :, :], d["bqk"]), (m.minus_k[:, :], d["minus_k"]), (m.minus_q[:, :], d["minus_q"]),
                    (m.ident16[:, :], d["ident16"]), (m.pick[:, :], d["pick"])]
    l1_values(nc, mem, d, m)
    scale_query_bias(nc, mem, m)
    l1_attention(nc, mem, d, m)
    c.ctx.close()
    transpose_rows(nc, mem, "att", m.ident, m.att, m.xnT)
    l1_output(nc, mem, d, m, m.xnT)
    b.ctx.close()
    a.ctx.close()


def scale_query_bias(nc, mem, m):
    s = mem.sem("query_bias_scaled")
    with nc.Block() as block:
        @block.vector
        def _(vec):
            nc.vector.tensor_scalar(m.bqk[:, 1, :], m.bqk[:, 1, :], float(HD) ** -0.5, None, ALU.mult).then_inc(s, 1)


PH = 8
KEYS = 64
TOP = 16
TABLE_ROWS = KEYS * KEYS
JJ = 32
RUNS = [(a, TOP // (a + 1)) for a in range(TOP)]
CAND = sum(n for _, n in RUNS)
FIRST = [sum(n for _, n in RUNS[:a]) for a in range(TOP)]
LOWEST = -3.0e38
HB = 4
PB = 16


def lookup_weights(nc, mem, d, m):
    t = Memory(nc, mem.sems)
    wq = t.sb("wq", [P, 2 * PH, C])
    keys = t.sb("keys", [P, 2 * PH, KEYS])
    ps = [t.ps(f"ps_wk{c}", [P, 2 * PH * KEYS]) for c in range(CC)]
    w_in, done, copied = mem.sem("lookup_in"), mem.sem("keys_joined"), mem.sem("keys_copied")
    with nc.Block() as block:
        @block.sync
        def _(sp):
            sp.dma_start(wq[:, :, :], d["pwq"].rearrange("(g p) c -> p g c", p=P)).then_inc(w_in, 16)
            sp.dma_start(keys[:, :, :], d["keysT"]).then_inc(w_in, 16)
            sp.dma_start(m.down[:, :, :, :], d["down"]).then_inc(w_in, 16)
            sp.dma_start(m.up[:, :, :], d["up"]).then_inc(w_in, 16)
            sp.dma_start(m.count[:, :, :], d["count"]).then_inc(w_in, 16)
            sp.wait_ge(w_in, 16 * 5)

        @block.tensor
        def _(pe):
            pe.wait_ge(w_in, 16 * 5)
            for c in range(CC):
                for g in range(2 * PH):
                    last = nc.tensor.matmul(ps[c][:, g * KEYS:(g + 1) * KEYS], wq[:, g, c * P:(c + 1) * P],
                                            keys[:, g, :], start=True, stop=True)
                last.then_inc(done, 1)

        @block.vector
        def _(vec):
            for c in range(CC):
                vec.wait_ge(done, c + 1)
                nc.vector.tensor_copy(m.wk[:, c, :], ps[c][:, :]).then_inc(copied, 1)
    t.ctx.close()


def lookup_experts(nc, mem, d, m):
    t = Memory(nc, mem.sems)
    xs, xh = t.sb("xs_t", [P, CC, P]), t.sb("xh_t", [P, CC, P])
    S, work = t.sb("S", [P, 2 * PH, KEYS]), t.sb("work", [P, 2 * PH, KEYS])
    val, idx = t.sb("val", [P, 2 * PH, TOP]), t.sb("idx", [P, 2 * PH, TOP], U32)
    code = t.sb("code", [P, 2 * PH, TOP])
    over = t.sb("over", [P, PH, TOP])
    cand, left = t.sb("cand", [P, PH, CAND]), t.sb("left", [P, PH, CAND])
    pay = t.sb("pay", [P, PH, CAND])
    best, pos = t.sb("best", [P, PH, TOP]), t.sb("pos", [P, PH, TOP], U32)
    pos16 = t.sb("pos16", [P, PH, TOP], F16)
    hit = t.sb("hit", [P, PH, CAND, TOP], F16)
    sel = t.sb("sel", [P, PH, CAND, TOP])
    e, den = t.sb("e", [P, PH, TOP]), t.sb("den", [P, PH])
    wgt = t.sb("wgt", [P, P])
    coden = t.sb("coden", [P, P], I32)
    code_r, code_c = t.sb("code_r", [P, P], I32), t.sb("code_c", [P, P], I32)
    rowf, colf = t.sb("rowf", [P, P]), t.sb("colf", [P, P])
    rowT, colT = t.sb("rowT", [P, P], F16), t.sb("colT", [P, P], F16)
    wT, whT, wlT = t.sb("wT", [P, P]), t.sb("whT", [P, P], F16), t.sb("wlT", [P, P], F16)
    A = t.sb("A", [P, P, P], F16)
    B = t.sb("B", [P, 2, JJ, P], F16)
    G = t.sb("G", [P, JJ, P])
    o_sb = t.sb("peer_o", [P, C])
    ps_s = t.ps("ps_sims", [P, 2 * PH * KEYS])
    ps_h = [t.ps(f"ps_down{b}", [P, HB, P]) for b in range(2)]
    ps_p = [t.ps(f"ps_pick{b}", [P, PB, JJ]) for b in range(2)]
    ps_o = t.ps("ps_up", [P, 512])
    ps_t = t.ps("ps_turn", [P, 4, P])
    NH, NP = JJ // HB, P // PB
    c_xs, c_xh = Count(mem, "xs_in", 16), Count(mem, "xh_in", 16)
    c_sims = Count(mem, "sims_summed", 1, 1)
    c_S = Count(mem, "sims_copied", 1)
    c_val = Count(mem, "keys_found", 1, 1)
    c_top = Count(mem, "pairs_found", 1, 1)
    c_pay = Count(mem, "rows_looked_up", 1, 1)
    c_e = Count(mem, "weights_exponential", 1)
    c_dec = Count(mem, "choice_decoded", 1, 1)
    c_turn = Count(mem, "choice_transposed", 1)
    c_tc = Count(mem, "choice_copied", 1, 1)
    c_ab = Count(mem, "one_hots_made", 1)
    c_h = Count(mem, "down_summed", NH)
    c_g = Count(mem, "gelu_done", NH, 2)
    c_p = Count(mem, "weights_spread", NP)
    c_w = Count(mem, "weights_applied", NP, 2)
    c_o = Count(mem, "up_summed", 1, 1)
    c_oc = Count(mem, "up_copied", 1, 1)
    c_k = Count(mem, "up_kept", 16, 16)
    chain, pchain = mem.sem("lookup_chain"), mem.sem("lookup_pool_chain")
    gates, pool_gates = mem.sem("lookup_gate"), mem.sem("lookup_pool_gate")
    peer_t = d["peer"].rearrange("(t p) c -> p t c", p=P)

    def wait(eng, c, i, k):
        v = c.at(i, k)
        if not isinstance(v, int) or v > 0:
            eng.wait_ge(c.sem, v)

    def stages(i, peeled):
        if not peeled:
            return True, True, True, True
        return i < NT, 1 <= i <= NT, i >= 2, i + 1 < NT

    def run(eng, step):
        step(0, True)
        step(1, True)
        with eng.Fori(2, NT - 1) as i:
            step(i, False)
        for i in range(NT - 1, NT + 2):
            step(i, True)

    with nc.Block() as block:
        @block.sync
        def _(sp):
            def load_xs(i):
                wait(sp, c_sims, i - 1, 1)
                sp.dma_start(xs[:, :, :], d["xgT"][:, :, bass.ds(i * P, P)]).then_inc(c_xs.sem, 16)

            def step(i, peeled):
                keys, spread, finish, ahead = stages(i, peeled)
                if finish:
                    wait(sp, c_o, i - 3, 1)
                    sp.dma_start(xh[:, :, :], d["xgT"][:, :, bass.ds((i - 2) * P, P)]).then_inc(c_xh.sem, 16)
                if ahead:
                    load_xs(i + 1)
                if finish:
                    wait(sp, c_oc, i - 2, 1)
                    sp.dma_start(peer_t[:, bass.ds(i - 2, 1), :], o_sb[:, :]).then_inc(c_k.sem, 16)

            sp.sem_inc(c_k.sem, 16)
            load_xs(0)
            run(sp, step)
            wait(sp, c_k, NT, 0)

        @block.tensor
        def _(pe):
            mm = nc.tensor.matmul
            pe.sem_inc(c_sims.sem, 1)
            pe.sem_inc(c_o.sem, 1)

            def sims(i):
                wait(pe, c_xs, i, 16)
                wait(pe, c_S, i - 1, 1)
                for h in range(2):
                    for c in range(CC):
                        last = mm(ps_s[:, h * 512:(h + 1) * 512], xs[:, c, :], m.wk[:, c, h * 512:(h + 1) * 512],
                                  start=(c == 0), stop=(c == CC - 1))
                last.then_inc(c_sims.sem, 1)

            def step(i, peeled):
                keys, spread, finish, ahead = stages(i, peeled)
                if spread:
                    wait(pe, c_dec, i - 1, 1)
                    wait(pe, c_tc, i - 2, 1)
                    for k, src in enumerate((rowf, colf, wgt)):
                        last = nc.tensor.transpose(ps_t[:, k, :], src[:, :], m.ident[:, :])
                    last.then_inc(c_turn.sem, 1)
                if finish:
                    wait(pe, c_xh, i - 2, 16)
                    for g in range(NH):
                        wait(pe, c_g, i - 2, g - 1)
                        for j in range(HB):
                            for c in range(CC):
                                last = mm(ps_h[g % 2][:, j, :], m.down[:, c, g * HB + j, :], xh[:, c, :],
                                          start=(c == 0), stop=(c == CC - 1))
                        last.then_inc(c_h.sem, 1)
                    wait(pe, c_ab, i - 2, 1)
                    for g in range(NP):
                        wait(pe, c_w, i - 2, g - 1)
                        for j in range(PB):
                            k = g * PB + j
                            for half in range(2):
                                last = mm(ps_p[g % 2][:, j, :], A[:, :, k], B[:, half, :, k],
                                          start=(half == 0), stop=(half == 1))
                        last.then_inc(c_p.sem, 1)
                if ahead:
                    sims(i + 1)
                if finish:
                    wait(pe, c_w, i - 2, NP)
                    wait(pe, c_oc, i - 3, 1)
                    for j in range(JJ):
                        last = mm(ps_o[:, 0:C], G[:, j, :], m.up[:, j, :], start=(j == 0), stop=(j == JJ - 1))
                    last.then_inc(c_o.sem, 1)

            sims(0)
            run(pe, step)

        @block.scalar
        def _(act):
            act.sem_inc(c_g.sem, c_g.credit)
            act.sem_inc(c_oc.sem, 1)

            def copy_sims(i):
                wait(act, c_sims, i, 1)
                wait(act, c_val, i - 1, 1)
                nc.scalar.copy(S[:, :, :], ps_s[:, :].rearrange("p (g k) -> p g k", k=KEYS)).then_inc(c_S.sem, 1)

            def step(i, peeled):
                keys, spread, finish, ahead = stages(i, peeled)
                if finish:
                    wait(act, c_o, i - 3, 1)
                    for g in range(NH):
                        wait(act, c_h, i - 2, g + 1)
                        nc.scalar.activation(G[:, g * HB:(g + 1) * HB, :], ps_h[g % 2][:, :, :],
                                             ACT.Gelu).then_inc(c_g.sem, 1)
                if ahead:
                    copy_sims(i + 1)
                if keys:
                    wait(act, c_top, i, 1)
                    nc.scalar.activation(e[:, :, :], e[:, :, :], ACT.Exp).then_inc(c_e.sem, 1)
                if finish:
                    wait(act, c_o, i - 2, 1)
                    wait(act, c_k, i - 2, 0)
                    nc.scalar.copy(o_sb[:, :], ps_o[:, 0:C]).then_inc(c_oc.sem, 1)

            copy_sims(0)
            run(act, step)

        @block.gpsimd
        def _(pool):
            pool.sem_inc(c_pay.sem, 1)
            ch = Chain(pool, pchain)
            PER = 9

            def step(i, peeled):
                keys, spread, finish, ahead = stages(i, peeled)
                if keys:
                    ch.enter(i, PER)
                    ch.base = i * PER
                    wait(pool, c_top, i, 1)
                    wait(pool, c_dec, i - 1, 1)
                    pool.sem_inc(pool_gates, 1)
                    tt = nc.gpsimd.tensor_tensor
                    ch.link(tt(sel[:, :, :, :], hit[:, :, :, :],
                               pay[:, :, :].unsqueeze(3).broadcast_to([P, PH, CAND, TOP]), ALU.mult))
                    n = CAND - CAND % 2
                    for w in (24, 12, 6, 3):
                        ch.link(tt(sel[:, :, 0:w, :], sel[:, :, 0:w, :], sel[:, :, w:2 * w, :], ALU.add))
                    for w in (1, 2, 48):
                        ch.link(tt(sel[:, :, 0, :], sel[:, :, 0, :], sel[:, :, w, :], ALU.add))
                    ch.link(tt(sel[:, :, 0, :], sel[:, :, 0, :], sel[:, :, 49, :], ALU.add))
                    pool.sem_inc(c_pay.sem, 1)
                    ch.n = 0

            run(pool, step)

        @block.vector
        def _(vec):
            v = nc.vector
            vec.sem_inc(c_val.sem, 1)
            vec.sem_inc(c_top.sem, 1)
            vec.sem_inc(c_dec.sem, 1)
            vec.sem_inc(c_tc.sem, 1)
            vec.sem_inc(c_w.sem, c_w.credit)
            ch = Chain(vec, chain)

            def decode(i):
                wait(vec, c_e, i, 1)
                ch.link(v.tensor_reduce(den[:, :], e[:, :, :], AXX, ALU.add))
                ch.link(v.reciprocal(den[:, :], den[:, :]))
                v.tensor_tensor(wgt[:, :].rearrange("p (n k) -> p n k", n=PH), e[:, :, :],
                                den[:, :].unsqueeze(2).broadcast_to([P, PH, TOP]), ALU.mult)
                wait(vec, c_pay, i, 1)
                ch.link(v.tensor_copy(coden[:, :].rearrange("p (n k) -> p n k", n=PH), sel[:, :, 0, :]))
                v.tensor_scalar(code_r[:, :], coden[:, :], 5, None, ALU.logical_shift_right)
                ch.link(v.tensor_scalar(code_c[:, :], coden[:, :], JJ - 1, None, ALU.bitwise_and))
                v.tensor_copy(rowf[:, :], code_r[:, :])
                ch.link(v.tensor_copy(colf[:, :], code_c[:, :]))
                vec.sem_inc(c_dec.sem, 1)

            def find(i):
                wait(vec, c_S, i, 1)
                vec.sem_inc(gates, 1)
                G2 = range(2 * PH)
                for g in G2:
                    last = v.max(out=val[:, g, 0:8], in_=S[:, g, :])
                ch.link(last)
                vec.sem_inc(gates, 1)
                for g in G2:
                    v.max_index(out=idx[:, g, 0:8], in_max=val[:, g, 0:8], in_values=S[:, g, :])
                    last = v.match_replace(out=work[:, g, :], in_to_replace=val[:, g, 0:8], in_values=S[:, g, :],
                                           imm_value=LOWEST)
                ch.link(last)
                vec.sem_inc(gates, 1)
                for g in G2:
                    last = v.max(out=val[:, g, 8:16], in_=work[:, g, :])
                ch.link(last)
                vec.sem_inc(gates, 1)
                for g in G2:
                    last = v.max_index(out=idx[:, g, 8:16], in_max=val[:, g, 8:16], in_values=work[:, g, :])
                ch.link(last)
                vec.sem_inc(c_val.sem, 1)
                v.tensor_scalar(code[:, 0:PH, :], idx[:, 0:PH, :], float(JJ), None, ALU.mult)
                ch.link(v.tensor_copy(code[:, PH:, :], idx[:, PH:, :]))
                ch.link(v.tensor_scalar(over[:, :, :], code[:, PH:, :], float(JJ), float(JJ * KEYS - JJ),
                                        ALU.is_ge, ALU.mult))
                ch.link(v.tensor_tensor(code[:, PH:, :], code[:, PH:, :], over[:, :, :], ALU.add))
                wait(vec, c_pay, i - 1, 1)
                for dst, src in ((cand, val), (pay, code)):
                    for a, n, rows in ((0, 16, 1), (1, 8, 1), (2, 5, 1), (3, 4, 1), (4, 3, 1), (5, 2, 3), (8, 1, 8)):
                        o = dst[:, :, FIRST[a]:FIRST[a] + n * rows].rearrange("p h (r n) -> p h r n", n=n)
                        last = v.tensor_tensor(
                            o, src[:, 0:PH, a:a + rows].unsqueeze(3).broadcast_to([P, PH, rows, n]),
                            src[:, PH:, 0:n].unsqueeze(2).broadcast_to([P, PH, rows, n]), ALU.add)
                ch.link(last)
                vec.sem_inc(gates, 1)
                for h in range(PH):
                    last = v.max(out=best[:, h, 0:8], in_=cand[:, h, :])
                ch.link(last)
                vec.sem_inc(gates, 1)
                for h in range(PH):
                    v.max_index(out=pos[:, h, 0:8], in_max=best[:, h, 0:8], in_values=cand[:, h, :])
                    last = v.match_replace(out=left[:, h, :], in_to_replace=best[:, h, 0:8], in_values=cand[:, h, :],
                                           imm_value=LOWEST)
                ch.link(last)
                vec.sem_inc(gates, 1)
                for h in range(PH):
                    last = v.max(out=best[:, h, 8:16], in_=left[:, h, :])
                ch.link(last)
                vec.sem_inc(gates, 1)
                for h in range(PH):
                    last = v.max_index(out=pos[:, h, 8:16], in_max=best[:, h, 8:16], in_values=left[:, h, :])
                ch.link(last)
                v.tensor_tensor(e[:, :, :], best[:, :, :], best[:, :, 0:1].broadcast_to([P, PH, TOP]), ALU.subtract)
                ch.link(v.tensor_copy(pos16[:, :, :], pos[:, :, :]))
                ch.link(v.tensor_tensor(hit[:, :, :, :],
                                        pos16[:, :, :].unsqueeze(2).broadcast_to([P, PH, CAND, TOP]),
                                        m.count[:, :, :].unsqueeze(1).broadcast_to([P, PH, CAND, TOP]), ALU.is_equal))
                vec.sem_inc(c_top.sem, 1)

            def apply(i):
                wait(vec, c_g, i, NH)
                for g in range(NP):
                    wait(vec, c_p, i, g + 1)
                    part = G[:, :, g * PB:(g + 1) * PB]
                    v.tensor_tensor(part, ps_p[g % 2][:, :, :].rearrange("p t j -> p j t"), part,
                                    ALU.mult).then_inc(c_w.sem, 1)

            def spread_out(i):
                wait(vec, c_turn, i, 1)
                v.tensor_copy(rowT[:, :], ps_t[:, 0, :])
                v.tensor_copy(colT[:, :], ps_t[:, 1, :])
                v.tensor_copy(wT[:, :], ps_t[:, 2, :])
                ch.link(v.tensor_copy(whT[:, :], ps_t[:, 2, :]))
                vec.sem_inc(c_tc.sem, 1)
                ch.link(v.tensor_tensor(wlT[:, :], wT[:, :], whT[:, :], ALU.subtract))
                wait(vec, c_p, i - 1, NP)
                for j in range(JJ):
                    last = v.tensor_scalar(B[:, 1, j, :], colT[:, :], float(j), None, ALU.is_equal)
                ch.link(last)
                for half, w in enumerate((whT, wlT)):
                    v.tensor_tensor(B[:, half, :, :], B[:, 1, :, :],
                                    w[:, :].unsqueeze(1).broadcast_to([P, JJ, P]), ALU.mult)
                for r in range(P):
                    last = v.tensor_scalar(A[:, r, :], rowT[:, :], float(r), None, ALU.is_equal)
                last.then_inc(c_ab.sem, 1)

            PER = {"decode": 5, "find": 14, "spread": 3}

            def step(i, peeled):
                keys, spread, finish, ahead = stages(i, peeled)
                if spread:
                    ch.n, ch.base = 0, i * 0 + dec_base(i)
                    decode(i - 1)
                    assert ch.n == PER["decode"], ch.n
                if keys:
                    ch.n, ch.base = 0, find_base(i)
                    find(i)
                    assert ch.n == PER["find"], ch.n
                if finish:
                    apply(i - 2)
                if spread:
                    ch.n, ch.base = 0, spread_base(i)
                    spread_out(i - 1)
                    assert ch.n == PER["spread"], ch.n

            FULL = sum(PER.values())

            def dec_base(i):
                return i * FULL + (PER["find"] - FULL)

            def find_base(i):
                return i * FULL + (PER["find"] + PER["decode"] - FULL) if not (isinstance(i, int) and i == 0) else 0

            def spread_base(i):
                if isinstance(i, int) and i == NT:
                    return dec_base(i) + PER["decode"]
                return i * FULL + (2 * PER["find"] + PER["decode"] - FULL)

            run(vec, step)
    t.ctx.close()


def last_combine(nc, mem, d, m):
    t = Memory(nc, mem.sems)
    H = NT // 2
    x, s, p = t.sb("fx", [P, H, C]), t.sb("fs", [P, H, C]), t.sb("fp", [P, H, C])
    x_in, gated, summed, stored = mem.sem("last_in"), mem.sem("last_gated"), mem.sem("last_summed"), mem.sem("stored")
    chain = mem.sem("last_chain")
    view = lambda a: a.rearrange("(t p) c -> p t c", p=P)
    with nc.Block() as block:
        @block.sync
        def _(sp):
            for k in range(2):
                if k:
                    sp.wait_ge(stored, 16)
                for dst, src in ((x, d["x1"]), (s, d["s1"]), (p, d["peer"])):
                    sp.dma_start(dst[:, :, :], view(src)[:, k * H:(k + 1) * H, :]).then_inc(x_in, 16)
                sp.wait_ge(summed, k + 1)
                sp.dma_start(view(d["out"])[:, k * H:(k + 1) * H, :], x[:, :, :]).then_inc(stored, 16)
            sp.wait_ge(stored, 32)

        @block.scalar
        def _(act):
            for k in range(2):
                act.wait_ge(x_in, 48 * (k + 1))
                nc.scalar.activation(p[:, :, :], p[:, :, :], ACT.Silu).then_inc(gated, 1)

        @block.vector
        def _(vec):
            ch = Chain(vec, chain)
            for k in range(2):
                vec.wait_ge(gated, k + 1)
                ch.link(nc.vector.tensor_tensor(s[:, :, :], s[:, :, :], p[:, :, :], ALU.mult))
                nc.vector.tensor_tensor(x[:, :, :], x[:, :, :], s[:, :, :], ALU.add).then_inc(summed, 1)
    t.ctx.close()


def rest(nc, mem, sems, d, m):
    layer1(nc, mem, sems, d, m)
    a = Memory(nc, sems)
    m.wk = a.sb("wk", [P, CC, 2 * PH * KEYS])
    m.down, m.up = a.sb("down", [P, CC, JJ, P]), a.sb("up", [P, JJ, C])
    m.count = a.sb("count", [P, CAND, TOP], F16)
    lookup_weights(nc, mem, d, m)
    lookup_experts(nc, mem, d, m)
    a.ctx.close()
    last_combine(nc, mem, d, m)


class Names:
    pass


def build(nc, d):
    with ExitStack() as sems:
        mem = Memory(nc, sems)
        m = Names()
        m.ident, m.ones, m.eps = mem.sb("ident", [P, P]), mem.sb("ones", [P, P]), mem.sb("eps", [P, 1])
        one = Memory(nc, sems)
        m.upto, m.expert_no = one.sb("upto", [P, P]), one.sb("expert_no", [P, E])
        m.tile_start = one.sb("tile_start", [P, ET])
        m.wconv, m.affw = one.sb("wconv", [P, CC]), one.sb("affw", [P, CC, 16])
        m.aff = one.sb("aff", [P, NT, 16])
        m.tok, m.sig, m.agv = one.sb("tok", [P, NT]), one.sb("sig", [P, NT]), one.sb("agv", [P, C])
        m.place, m.tile_expert = one.sb("place", [P, NT], U32), one.sb("tile_expert", [1, ET], I32)
        m.xn = one.sb("xn", [P, NT, C])
        two = Memory(nc, sems)
        m.xh = two.sb("xh", [P, NT, C])
        three = Memory(nc, sems)
        m.xnT = three.sb("xnT", [P, CC, N])
        m.wqkv, m.wqkvT = three.sb("wqkv", [P, 3 * CC, C]), three.sb("wqkvT", [P, CC, 3 * C])
        m.l0_loads = [
            (m.wqkv[:, :, :], d["wqkv"].rearrange("(k p) c -> p k c", p=P)),
            (m.wqkvT[:, :, :], d["wqkvT"].rearrange("(k p) c -> p k c", p=P)),
            (m.wconv[:, :], d["wconv"]),
            (m.affw[:, :, 0:E], d["centT"].rearrange("(k p) e -> p k e", p=P)),
        ]
        l0_normalise(nc, mem, d, m)
        transpose_rows(nc, mem, "xn0", m.ident, m.xn, m.xnT)
        l0_global_attention(nc, mem, d, m)
        three.ctx.close()
        l0_route(nc, mem, d, m)
        two.ctx.close()
        l0_experts(nc, mem, d, m)
        l0_combine(nc, mem, d, m)
        one.ctx.close()
        rest(nc, mem, sems, d, m)
        mem.ctx.close()

SCRATCH = {"sorted_x": (ET * P, C), "sorted_y": (ET * P, C), "x1": (N, C), "xgT": (P, CC, N), "s1": (N, C),
           "peer": (N, C)}


def extra_inputs(host, w, _np):
    host["gamma"] = w["L1_ffn_gamma"].reshape(CC, P).T
    host["wv"], host["wo"] = w["L1_attn_Wv"], w["L1_attn_Wo"]
    host["bv"], host["bo"] = w["L1_attn_bv"].reshape(1, C), w["L1_attn_bo"].reshape(1, C)

    def rows_of(a, low):
        by_head = a.reshape(a.shape[:-1] + (PAIRS, 2, HD))
        out = _np.zeros(a.shape[:-1] + (PAIRS, 2, ROWS), a.dtype)
        for r in (0, HD, LO):
            out[..., r:r + HD] = by_head
        return out.reshape(a.shape[:-1] + (PAIRS, P))

    wq, wk = rows_of(w["L1_attn_Wq"], 0), rows_of(w["L1_attn_Wk"], 0)
    wqk = _np.stack([wk, wq])
    host["wqk"] = wqk.reshape(2, CC, P, PAIRS, P).transpose(3, 2, 0, 1, 4)
    host["bqk"] = _np.stack([rows_of(w["L1_attn_bk"], 0), rows_of(w["L1_attn_bq"], 0)]).transpose(2, 0, 1)
    f16, f32 = _np.float16, _np.float32
    mk, mq = _np.zeros((2, ROWS), f32), _np.zeros((2, ROWS), f32)
    mk[:, HD:2 * HD] = -1.0
    mq[:, LO:LO + HD] = -1.0
    host["minus_k"], host["minus_q"] = mk.reshape(P, 1), mq.reshape(P, 1)
    slope = (_np.float32(2.0 ** (-8.0 / H)) ** _np.arange(1, H + 1, dtype=f32)).astype(f32)
    pos = _np.arange(N, dtype=f32)

    def halves(a):
        hi = a.astype(f16)
        return hi, (a - hi.astype(f32)).astype(f16)

    sh, sl = halves(slope)
    host["slopes"] = _np.broadcast_to(_np.stack([sh, sl], 1), (P, H, 2))
    host["start"] = _np.broadcast_to((slope[:, None] * (_np.arange(NQ) * QB) / MSCALE).astype(f32), (P, H, NQ))
    rel = (_np.arange(GK * NQ) - GK * (NQ - 1)) * (GK * P)
    host["abias"] = (slope[None, :, None] * (_np.arange(P)[:, None, None] + rel[None, None, :])).astype(f32)
    kspec = _np.zeros((H, NSPEC, N), f16)
    kspec[:, 0:2] = MSCALE
    kspec[:, 2:4] = (P * ((pos // P) % GK)).astype(f16)
    kspec[:, 4], kspec[:, 5] = halves(slope[:, None] * pos[None, :])
    host["kspec"] = kspec.reshape(PAIRS, 2, NSPEC, N)
    qspec = _np.zeros((NSPEC, N), f16)
    qspec[4:6] = 1.0
    host["qspec"] = qspec
    host["ident16"] = _np.eye(P, dtype=f16)
    pick = _np.zeros((2, GK, 32, 2, HD + 1), f32)
    for h in range(2):
        for r in range(HD + 1):
            pick[h, :, r, h, r] = 1.0
    host["pick"] = pick.reshape(P, 2 * (HD + 1))
    host["pwq"] = w["L1_ffn_wq"]
    host["keysT"] = w["L1_ffn_keys"].transpose(3, 2, 0, 1).reshape(P, 2 * PH, KEYS)
    def by_tile(a):
        return a[:TABLE_ROWS].reshape(KEYS, 2, JJ, C).transpose(2, 1, 0, 3).reshape(JJ, P, C)

    down = by_tile(w["L1_ffn_table_down"])
    host["down"] = down.reshape(JJ, P, CC, P).transpose(3, 2, 0, 1)
    host["up"] = by_tile(w["L1_ffn_table_up"]).transpose(1, 0, 2)
    host["count"] = _np.broadcast_to(_np.arange(CAND, dtype=f16)[None, :, None], (P, CAND, TOP))


def kernel(**inputs):
    import numpy as _np
    import concourse.bacc as _bacc
    from concourse import mybir as _mybir
    from concourse.bass_utils import run_bass_kernel_spmd as _run

    w = {k: _np.asarray(v) for k, v in inputs.items()}
    e, f, c = w["L0_ffn_w1"].shape

    def columns(a):
        return _np.moveaxis(a.reshape(a.shape[:-1] + (a.shape[-1] // P, P)), -1, 0)

    table = _np.concatenate([columns(w[k]) for k in ("L0_ffn_ln_g", "L0_ffn_ln_b", "L0_ffn_b1")], axis=2)
    host = {
        "x": w["L0_attn_x"].reshape(N, C),
        "wqkv": w["L0_attn_w_qkv"], "wqkvT": w["L0_attn_w_qkv"].T,
        "wconv": columns(w["L0_attn_w_conv1"]),
        "centT": w["L0_ffn_centroids"].T,
        "table": table.transpose(1, 0, 2),
        "w1": w["L0_ffn_w1"].reshape(e, f, CC, P).transpose(0, 3, 2, 1),
        "w2": w["L0_ffn_w2"].reshape(e, c, FC, P).transpose(0, 3, 2, 1),
        "b2": w["L0_ffn_b2"],
    }
    extra_inputs(host, w, _np)
    nc = _bacc.Bacc("TRN2", target_bir_lowering=False, num_devices=1)
    arrays, drams = {}, {}
    for name, a in host.items():
        a = _np.ascontiguousarray(a)
        arrays[f"in_{name}"] = a
        drams[name] = nc.dram_tensor(f"in_{name}", a.shape, _mybir.dt.from_np(a.dtype), kind="ExternalInput").ap()
    drams["out"] = nc.dram_tensor("out", (N, C), F32, kind="ExternalOutput").ap()
    for name, shape in SCRATCH.items():
        drams[name] = nc.dram_tensor(name, shape, F32, kind="Internal").ap()
    build(nc, drams)
    r = _run(nc, [arrays], core_ids=[0])
    return r.results[0]["out"].reshape(1, N, C)
```

```python
import numpy as np
import concourse.bass as bass
from concourse import mybir
from contextlib import ExitStack

F32, F16, BF16 = mybir.dt.float32, mybir.dt.float16, mybir.dt.bfloat16
U32, I32 = mybir.dt.uint32, mybir.dt.int32
ALU = mybir.AluOpType
ACT = mybir.ActivationFunctionType
AXX = mybir.AxisListType.X

P = 128
N = 4096
C = 256
NT = N // P
CC = C // P
EPS = 1e-5
E = 8
F = 1024
FC = F // P
ET = NT + E
TABLE = 2 * CC + FC


class Chain:

    def __init__(self, eng, sem):
        self.eng, self.sem, self.n, self.base = eng, sem, 0, 0

    def link(self, ins):
        self.n += 1
        ins.then_inc(self.sem, 1)
        self.eng.wait_ge(self.sem, self.base + self.n)

    def enter(self, i, per_step):
        self.outer, self.per_step = self.n, per_step
        self.base, self.n = i * per_step + self.outer, 0

    def leave(self, steps):
        assert self.n == self.per_step, (self.n, self.per_step)
        self.base, self.n = 0, self.outer + steps * self.per_step


class Memory:

    def __init__(self, nc, sems):
        self.nc, self.sems, self.ctx = nc, sems, ExitStack()

    def sb(self, name, shape, dt=F32):
        return self.ctx.enter_context(self.nc.sbuf_tensor(name, shape, dt))

    def ps(self, name, shape, dt=F32):
        return self.ctx.enter_context(self.nc.psum_tensor(name, shape, dt))

    def sem(self, name):
        return self.sems.enter_context(self.nc.semaphore(name))


def row_statistics(nc, vec, ch, src, stats, mv, given):
    with vec.Fori(0, NT) as i:
        nc.vector.bn_stats(stats[:, bass.ds(i, 1), :], src[:, bass.ds(i, 1), :]).then_inc(ch.sem, 1)
    ch.n += NT
    vec.wait_ge(ch.sem, ch.n)
    for i in range(NT):
        nc.vector.bn_aggr(mv[:, i, :], stats[:, i, :]).then_inc(given, 1)


def apply_statistics(nc, vec, ch, src, dst, mv, rstd):
    with vec.Fori(0, NT) as i:
        nc.vector.tensor_scalar(dst[:, bass.ds(i, 1), :], src[:, bass.ds(i, 1), :],
                                mv[:, bass.ds(i, 1), 0:1], rstd[:, bass.ds(i, 1)],
                                ALU.subtract, ALU.mult).then_inc(ch.sem, 1)
    ch.n += NT
    vec.wait_ge(ch.sem, ch.n)


def transpose_rows(nc, mem, tag, ident, src, dst):
    done = mem.sem(f"{tag}_transposed")
    copied = [mem.sem(f"{tag}_copied_dve"), mem.sem(f"{tag}_copied_act")]
    ps = Memory(nc, mem.sems)
    bank = [ps.ps(f"{tag}_ps{b}", [P, 4 * P]) for b in range(4)]
    groups = [(c, g) for g in range(NT // 4) for c in range(CC)]
    with nc.Block() as block:
        @block.tensor
        def _(pe):
            for k, (c, g) in enumerate(groups):
                if k >= 4:
                    pe.wait_ge(copied[k % 2], (k - 4) // 2 + 1)
                for t in range(4):
                    last = nc.tensor.transpose(bank[k % 4][:, t * P:(t + 1) * P],
                                               src[:, 4 * g + t, c * P:(c + 1) * P], ident[:, :])
                last.then_inc(done, 1)

        def take(eng, copy, half):
            for k, (c, g) in enumerate(groups):
                if k % 2 == half:
                    eng.wait_ge(done, k + 1)
                    copy(dst[:, c, g * 4 * P:(g + 1) * 4 * P], bank[k % 4][:, :]).then_inc(copied[half], 1)

        @block.vector
        def _(vec):
            take(vec, nc.vector.tensor_copy, 0)

        @block.scalar
        def _(act):
            take(act, nc.scalar.copy, 1)
    ps.ctx.close()


def l0_normalise(nc, mem, d, m):
    t = Memory(nc, mem.sems)
    X = t.sb("X", [P, NT, C])
    stats, mv = t.sb("stats", [P, NT, 6]), t.sb("mv", [P, NT, 2])
    sd, rstd = t.sb("sd", [P, NT]), t.sb("rstd", [P, NT])
    x_in, given = mem.sem("x_in"), mem.sem("statistics_given")
    rooted, ones_in = mem.sem("deviation_given"), mem.sem("constants_made")
    chain = mem.sem("l0_norm_chain")
    with nc.Block() as block:
        @block.sync
        def _(sp):
            sp.dma_start(X[:, :, :], d["x"].rearrange("(t p) c -> p t c", p=P)).then_inc(x_in, 16)
            for dst, src in m.l0_loads:
                sp.dma_start(dst, src).then_inc(x_in, 16)
            sp.wait_ge(x_in, 16 * (1 + len(m.l0_loads)))

        @block.gpsimd
        def _(pool):
            nc.gpsimd.memset(m.ident[:, :], 0.0).then_inc(ones_in, 1)
            nc.gpsimd.memset(m.ones[:, :], 1.0).then_inc(ones_in, 1)
            nc.gpsimd.memset(m.upto[:, :], 1.0).then_inc(ones_in, 1)
            nc.gpsimd.memset(m.eps[:, :], EPS).then_inc(ones_in, 1)
            pool.wait_ge(ones_in, 4)
            nc.gpsimd.affine_select(out=m.ident[:, :], in_=m.ident[:, :], compare_op=ALU.not_equal, fill=1.0,
                                    base=0, pattern=[[-1, P]], channel_multiplier=1).then_inc(ones_in, 1)
            nc.gpsimd.affine_select(out=m.upto[:, :], in_=m.upto[:, :], compare_op=ALU.is_ge, fill=0.0,
                                    base=0, pattern=[[1, P]], channel_multiplier=-1).then_inc(ones_in, 1)
            nc.gpsimd.iota(m.expert_no[:, :], [[1, E]], base=0, channel_multiplier=0,
                           allow_small_or_imprecise_dtypes=True).then_inc(ones_in, 1)
            nc.gpsimd.iota(m.tile_start[:, :], [[P, ET]], base=0, channel_multiplier=0,
                           allow_small_or_imprecise_dtypes=True).then_inc(ones_in, 1)

        @block.vector
        def _(vec):
            ch = Chain(vec, chain)
            vec.wait_ge(x_in, 16 * (1 + len(m.l0_loads)))
            for n, (src, dst) in enumerate(((X, m.xn), (m.xn, m.xh))):
                row_statistics(nc, vec, ch, src, stats, mv, given)
                vec.wait_ge(rooted, n + 1)
                ch.link(nc.vector.reciprocal(rstd[:, :], sd[:, :]))
                apply_statistics(nc, vec, ch, src, dst, mv, rstd)

        @block.scalar
        def _(act):
            act.wait_ge(ones_in, 8)
            for n in range(2):
                act.wait_ge(given, NT * (n + 1))
                nc.scalar.activation(sd[:, :], mv[:, :, 1], ACT.Sqrt, bias=m.eps[:, :]).then_inc(rooted, 1)
    t.ctx.close()


def l0_global_attention(nc, mem, d, m):
    t = Memory(nc, mem.sems)
    yz = t.sb("yz", [P, CC])
    row = t.sb("row", [1, C])
    erow = t.sb("erow", [1, C])
    small = t.sb("small", [P, 8])
    prow = t.sb("prow", [1, P])
    acol, ucol = t.sb("acol", [P, CC]), t.sb("ucol", [P, CC])
    e_n, w_n = t.sb("e_n", [P, NT]), t.sb("w_n", [P, NT])
    zwide = t.sb("zwide", [P, CC, P])
    ps_a = t.ps("ps_a", [P, NT, 16])
    ps_b = t.ps("ps_b", [P, 512])
    ps_c = t.ps("ps_c", [P, 512])
    s = mem.sem("pe_to_dve")
    v = mem.sem("dve_to_pe")
    a_in, a_out = mem.sem("exp_in_ready"), mem.sem("exp_done")
    chain = mem.sem("l0_attn_chain")
    wq, wk, wv = (slice(i * C, (i + 1) * C) for i in range(3))
    with nc.Block() as block:
        @block.tensor
        def _(pe):
            mm = nc.tensor.matmul
            for c in range(CC):
                for k in range(CC):
                    last = mm(ps_b[:, c:c + 1], m.wqkv[:, k, c * P:(c + 1) * P], m.wconv[:, k:k + 1],
                              start=(k == 0), stop=(k == CC - 1))
            last.then_inc(s, 1)
            pe.wait_ge(v, 1)
            for i in range(NT):
                for c in range(CC):
                    last = mm(ps_a[:, i, 0:E + 1], m.xnT[:, c, i * P:(i + 1) * P], m.affw[:, c, 0:E + 1],
                              start=(c == 0), stop=(c == CC - 1))
            last.then_inc(s, 1)
            pe.wait_ge(v, 2)
            for c in range(CC):
                for i in range(NT):
                    last = mm(ps_b[:, c:c + 1], m.xn[:, i, c * P:(c + 1) * P], m.aff[:, i, E:E + 1],
                              start=(i == 0), stop=(i == NT - 1))
            last.then_inc(s, 1)
            pe.wait_ge(v, 3)
            for c in range(CC):
                last = mm(ps_c[0:1, 0:C], yz[:, c:c + 1], m.wqkvT[:, c, wk], start=(c == 0), stop=(c == CC - 1))
            last.then_inc(s, 1)
            pe.wait_ge(v, 4)
            for k in range(CC):
                last = mm(ps_b[:, k:k + 1], row[0:1, k * P:(k + 1) * P], m.ones[0:1, 0:1], start=True, stop=True)
            last.then_inc(s, 1)
            pe.wait_ge(v, 5)
            for c in range(CC):
                for k in range(CC):
                    last = mm(ps_b[:, c:c + 1], m.wqkv[:, 2 * CC + k, c * P:(c + 1) * P], acol[:, k:k + 1],
                              start=(k == 0), stop=(k == CC - 1))
            last.then_inc(s, 1)
            pe.wait_ge(v, 6)
            for i in range(NT):
                for c in range(CC):
                    last = mm(ps_a[:, i, 0:1], m.xnT[:, c, i * P:(i + 1) * P], ucol[:, c:c + 1],
                              start=(c == 0), stop=(c == CC - 1))
            last.then_inc(s, 1)
            pe.wait_ge(v, 7)
            nc.tensor.transpose(ps_b[0:1, 0:P], small[:, 0:1], m.ident[:, :]).then_inc(s, 1)
            pe.wait_ge(v, 8)
            mm(ps_c[:, 0:1], m.ones[0:1, :], small[0:1, 2:3], start=True, stop=True).then_inc(s, 1)
            pe.wait_ge(a_out, 3)
            mm(ps_b[:, 0:1], m.ones[:, :], small[:, 4:5], start=True, stop=True).then_inc(s, 1)
            pe.wait_ge(v, 9)
            for c in range(CC):
                for i in range(NT):
                    last = mm(ps_c[:, c:c + 1], m.xn[:, i, c * P:(c + 1) * P], w_n[:, i:i + 1],
                              start=(i == 0), stop=(i == NT - 1))
            last.then_inc(s, 1)
            pe.wait_ge(v, 10)
            for c in range(CC):
                last = mm(ps_b[:, 0:C], zwide[:, c, :], m.wqkvT[:, c, wv], start=(c == 0), stop=(c == CC - 1))
            last.then_inc(s, 1)

        @block.vector
        def _(vec):
            ch = Chain(vec, chain)
            vec.wait_ge(s, 1)
            nc.vector.tensor_copy(m.affw[:, :, E], ps_b[:, 0:CC]).then_inc(v, 1)
            vec.wait_ge(s, 2)
            ch.link(nc.vector.tensor_copy(m.aff[:, :, 0:E + 1], ps_a[:, :, 0:E + 1]))
            nc.vector.tensor_tensor(m.tok[:, :], m.aff[:, :, E], m.aff[:, :, E], ALU.subtract).then_inc(v, 1)
            vec.wait_ge(s, 3)
            nc.vector.tensor_scalar(yz[:, :], ps_b[:, 0:CC], float(C) ** -0.5, None, ALU.mult).then_inc(v, 1)
            vec.wait_ge(s, 4)
            nc.vector.tensor_reduce(small[0:1, 5:6], ps_c[0:1, 0:C], AXX, ALU.max, negate=True).then_inc(a_in, 1)
            vec.wait_ge(a_out, 2)
            ch.link(nc.vector.reciprocal(small[0:1, 7:8], small[0:1, 6:7]))
            nc.vector.tensor_scalar(row[0:1, :], erow[0:1, :], small[0:1, 7:8], None, ALU.mult).then_inc(v, 1)
            vec.wait_ge(s, 5)
            nc.vector.tensor_copy(acol[:, :], ps_b[:, 0:CC]).then_inc(v, 1)
            vec.wait_ge(s, 6)
            nc.vector.tensor_copy(ucol[:, :], ps_b[:, 0:CC]).then_inc(v, 1)
            vec.wait_ge(s, 7)
            ch.link(nc.vector.tensor_reduce(small[:, 0:1], ps_a[:, :, 0], AXX, ALU.max))
            nc.vector.tensor_copy(e_n[:, :], ps_a[:, :, 0]).then_inc(v, 1)
            vec.wait_ge(s, 8)
            nc.vector.tensor_reduce(small[0:1, 2:3], ps_b[0:1, 0:P], AXX, ALU.max, negate=True).then_inc(v, 1)
            vec.wait_ge(s, 9)
            nc.vector.tensor_copy(small[:, 3:4], ps_c[:, 0:1]).then_inc(a_in, 1)
            vec.wait_ge(s, 10)
            ch.link(nc.vector.reciprocal(small[:, 1:2], ps_b[:, 0:1]))
            nc.vector.tensor_scalar(w_n[:, :], e_n[:, :], small[:, 1:2], None, ALU.mult).then_inc(v, 1)
            vec.wait_ge(s, 11)
            nc.vector.tensor_copy(zwide[:, :, :], ps_c[:, 0:CC].unsqueeze(2).broadcast_to([P, CC, P])).then_inc(v, 1)
            ch.link(nc.vector.reciprocal(m.sig[:, :], m.tok[:, :]))
            ch.link(nc.vector.tensor_tensor(m.tok[:, :], m.tok[:, :], m.sig[:, :], ALU.mult))
            vec.wait_ge(s, 12)
            ch.link(nc.vector.tensor_copy(m.agv[:, :], ps_b[:, 0:C]))

        @block.scalar
        def _(act):
            act.wait_ge(v, 2)
            nc.scalar.activation(m.tok[:, :], m.tok[:, :], ACT.Exp).then_inc(a_out, 1)
            act.wait_ge(a_in, 1)
            nc.scalar.activation(erow[0:1, :], ps_c[0:1, 0:C], ACT.Exp, bias=small[0:1, 5:6],
                                 accum_out=small[0:1, 6:7]).then_inc(a_out, 1)
            act.wait_ge(a_in, 2)
            nc.scalar.activation(e_n[:, :], e_n[:, :], ACT.Exp, bias=small[:, 3:4],
                                 accum_out=small[:, 4:5]).then_inc(a_out, 1)
    t.ctx.close()


def l0_route(nc, mem, d, m):
    t = Memory(nc, mem.sems)
    top, arg = t.sb("top", [P, NT, 8]), t.sb("arg", [P, NT, 8], U32)
    argf = t.sb("argf", [P, NT])
    hot = t.sb("hot", [P, NT, E])
    rank = t.sb("rank", [P, NT, E])
    tot = t.sb("tot", [P, E, NT + 1])
    scan = t.sb("scan", [P, E, NT + 1])
    zero = t.sb("zero", [P, E, NT + 1])
    cnt, cnti = t.sb("cnt", [P, E]), t.sb("cnti", [P, E], I32)
    posf = t.sb("posf", [P, NT])
    blank = t.sb("blank", [P, C * 8])
    tile_e = t.sb("tile_e", [1, ET])
    ps = t.ps("ps_route", [P, 2, 512])
    hot_given, summed = mem.sem("one_hot_given"), mem.sem("prefix_summed")
    placed, blanked, scattered = mem.sem("places_given"), mem.sem("rows_blanked"), mem.sem("rows_scattered")
    zeroed, sig_in, sig_out = mem.sem("zeroed"), mem.sem("sigmoid_in"), mem.sem("sigmoid_out")
    chain = mem.sem("route_chain")
    with nc.Block() as block:
        @block.vector
        def _(vec):
            ch = Chain(vec, chain)
            ch.link(nc.vector.memset(blank[:, :], 0.0))
            nc.vector.memset(zero[:, :, :], 0.0).then_inc(zeroed, 1)
            for i in range(NT):
                last = nc.vector.max(out=top[:, i, :], in_=m.aff[:, i, 0:E])
            ch.link(last)
            nc.vector.tensor_copy(m.sig[:, :], top[:, :, 0]).then_inc(sig_in, 1)
            for i in range(NT):
                last = nc.vector.max_index(out=arg[:, i, :], in_max=top[:, i, :], in_values=m.aff[:, i, 0:E])
            ch.link(last)
            ch.link(nc.vector.tensor_copy(argf[:, :], arg[:, :, 0]))
            ch.link(nc.vector.tensor_tensor(hot[:, :, :], argf[:, :].unsqueeze(2).broadcast_to([P, NT, E]),
                                            m.expert_no[:, :].unsqueeze(1).broadcast_to([P, NT, E]), ALU.is_equal))
            vec.sem_inc(hot_given, 1)
            vec.wait_ge(summed, 1)
            ch.link(nc.vector.tensor_copy(tot[:, :, 0:NT], ps[:, 1, 0:NT * E].rearrange("p (t e) -> p e t", e=E)))
            ch.link(nc.vector.tensor_copy(rank[:, :, :], ps[:, 0, 0:NT * E].rearrange("p (t e) -> p t e", e=E)))
            ch.link(nc.vector.tensor_reduce(cnt[:, :], tot[:, :, 0:NT], AXX, ALU.add))
            ch.link(nc.vector.tensor_scalar(cnti[:, :], cnt[:, :], float(P - 1), None, ALU.add))
            ch.link(nc.vector.tensor_scalar(cnti[:, :], cnti[:, :], 7, 7, ALU.logical_shift_right,
                                            ALU.logical_shift_left))
            ch.link(nc.vector.tensor_copy(tot[:, :, NT], cnti[:, :]))
            ch.link(nc.vector.tensor_tensor(tot[:, :, NT], tot[:, :, NT], cnt[:, :], ALU.subtract))
            flat = lambda a: a[:, :, :].rearrange("p e t -> p (e t)")
            ch.link(nc.vector.tensor_tensor_scan(flat(scan), flat(tot), flat(zero), 0.0, ALU.add, ALU.add))
            ch.link(nc.vector.memset(tile_e[0:1, :], 0.0))
            for e in range(E - 1):
                ch.link(nc.vector.scalar_tensor_tensor(tile_e[0:1, :], m.tile_start[0:1, :],
                                                       scan[0:1, e, NT:NT + 1], tile_e[0:1, :],
                                                       ALU.is_ge, ALU.add))
            ch.link(nc.vector.tensor_copy(m.tile_expert[0:1, :], tile_e[0:1, :]))
            ch.link(nc.vector.tensor_tensor(scan[:, :, :], scan[:, :, :], tot[:, :, :], ALU.subtract))
            ch.link(nc.vector.tensor_tensor(rank[:, :, :], rank[:, :, :],
                                            scan[:, :, 0:NT].rearrange("p e t -> p t e"), ALU.add))
            ch.link(nc.vector.tensor_tensor(rank[:, :, :], rank[:, :, :], hot[:, :, :], ALU.mult))
            ch.link(nc.vector.tensor_reduce(posf[:, :], rank[:, :, :], AXX, ALU.add))
            ch.link(nc.vector.tensor_scalar(m.place[:, :], posf[:, :], -1.0, None, ALU.add))
            vec.sem_inc(placed, 1)
            vec.wait_ge(sig_out, 1)
            ch.link(nc.vector.tensor_scalar(m.sig[:, :], m.sig[:, :], 1.0, None, ALU.add))
            ch.link(nc.vector.reciprocal(m.sig[:, :], m.sig[:, :]))

        @block.scalar
        def _(act):
            act.wait_ge(sig_in, 1)
            nc.scalar.activation(m.sig[:, :], m.sig[:, :], ACT.Exp, scale=-1.0).then_inc(sig_out, 1)

        @block.tensor
        def _(pe):
            pe.wait_ge(hot_given, 1)
            flat = hot[:, :, :].rearrange("p t e -> p (t e)")
            nc.tensor.matmul(ps[:, 0, 0:NT * E], m.upto[:, :], flat, start=True, stop=True)
            nc.tensor.matmul(ps[:, 1, 0:NT * E], m.ones[:, :], flat, start=True, stop=True).then_inc(summed, 1)

        @block.sync
        def _(sp):
            sp.wait_ge(zeroed, 1)
            for k in range(ET // 8):
                sp.dma_start(d["sorted_x"][k * 8 * P:(k + 1) * 8 * P, :].rearrange("(p r) c -> p (r c)", p=P),
                             blank[:, :]).then_inc(blanked, 16)
            sp.wait_ge(blanked, 16 * (ET // 8))

        @block.gpsimd
        def _(pool):
            pool.wait_ge(placed, 1)
            pool.wait_ge(blanked, 16 * (ET // 8))
            for i in range(NT):
                nc.gpsimd.indirect_dma_start(
                    out=d["sorted_x"], out_offset=bass.IndirectOffsetOnAxis(ap=m.place[:, i:i + 1], axis=0),
                    in_=m.xh[:, i, :], in_offset=None).then_inc(scattered, 16)
            pool.wait_ge(scattered, 16 * NT)
    t.ctx.close()


def l0_experts(nc, mem, d, m):
    t = Memory(nc, mem.sems)
    B = 2
    xs = [t.sb(f"xs{b}", [P, C]) for b in range(B)]
    w1 = [t.sb(f"w1{b}", [P, CC, F]) for b in range(B)]
    w2 = [t.sb(f"w2{b}", [P, FC, C]) for b in range(B)]
    tab = [t.sb(f"tab{b}", [P, TABLE]) for b in range(B)]
    b2 = [t.sb(f"b2{b}", [1, C]) for b in range(B)]
    xe = [t.sb(f"xe{b}", [P, CC, P]) for b in range(B)]
    h = [t.sb(f"h{b}", [P, FC, P]) for b in range(B)]
    y = [t.sb(f"y{b}", [P, C]) for b in range(B)]
    ps_t = [t.ps(f"ps_t{b}", [P, 512]) for b in range(B)]
    ps_h = [t.ps(f"ps_h{b}", [P, 2, 4 * P]) for b in range(B)]
    ps_y = t.ps("ps_y", [P, B, C])
    sem = lambda s: [mem.sem(f"{s}{b}") for b in range(B)]
    loaded = sem("expert_loaded")
    turned, shifted = sem("tile_transposed"), sem("tile_shifted")
    up, relu_v, relu_a = sem("hidden_summed"), sem("relu_dve"), sem("relu_act")
    down, copied, stored = sem("output_summed"), sem("output_copied"), sem("output_stored")
    LOADS = 5
    steps = ET // B
    with nc.Block() as block:
        @block.sync
        def _(sp):
            with sp.Fori(0, steps) as i:
                for b in range(B):
                    j = i * B + b
                    sp.wait_ge(down[b], i + 1)
                    e = sp.value_load(m.tile_expert[0:1, bass.ds(j, 1)], min_val=0, max_val=E - 1)
                    sp.dma_start(xs[b][:, :], d["sorted_x"][bass.ds(j * P, P), :]).then_inc(loaded[b], 16)
                    sp.dma_start(tab[b][:, :], d["table"][bass.ds(e, 1), :, :]).then_inc(loaded[b], 16)
                    sp.dma_start(b2[b][:, :], d["b2"][bass.ds(e, 1), :]).then_inc(loaded[b], 16)
                    sp.dma_start(w1[b][:, :, :], d["w1"][bass.ds(e, 1), :, :, :]).then_inc(loaded[b], 16)
                    sp.dma_start(w2[b][:, :, :], d["w2"][bass.ds(e, 1), :, :, :]).then_inc(loaded[b], 16)

        @block.tensor
        def _(pe):
            mm = nc.tensor.matmul
            for b in range(B):
                pe.sem_inc(down[b], 1)
            with pe.Fori(0, steps) as i:
                for b in range(B):
                    pe.wait_ge(loaded[b], (i + 1) * 16 * LOADS)
                    for c in range(CC):
                        last = nc.tensor.transpose(ps_t[b][:, c * P:(c + 1) * P], xs[b][:, c * P:(c + 1) * P],
                                                   m.ident[:, :])
                    last.then_inc(turned[b], 1)
                    pe.wait_ge(shifted[b], i + 1)
                    for f in range(FC):
                        for c in range(CC):
                            last = mm(ps_h[b][:, f // 4, (f % 4) * P:(f % 4 + 1) * P],
                                      w1[b][:, c, f * P:(f + 1) * P], xe[b][:, c, :],
                                      start=(c == 0), stop=(c == CC - 1))
                        if f % 4 == 3:
                            last.then_inc(up[b], 1)
                    pe.wait_ge(copied[b], i + 1)
                    mm(ps_y[:, b, :], m.ones[0:1, :], b2[b][0:1, :], start=True, stop=False)
                    pe.wait_ge(relu_v[b], i + 1)
                    for f in range(FC):
                        if f == 4:
                            pe.wait_ge(relu_a[b], i + 1)
                        last = mm(ps_y[:, b, :], h[b][:, f, :], w2[b][:, f, :], start=False, stop=(f == FC - 1))
                    last.then_inc(down[b], 1)

        @block.vector
        def _(vec):
            for b in range(B):
                vec.sem_inc(copied[b], 1)
            with vec.Fori(0, steps) as i:
                for b in range(B):
                    vec.wait_ge(turned[b], i + 1)
                    for c in range(CC):
                        last = nc.vector.tensor_scalar(xe[b][:, c, :], ps_t[b][:, c * P:(c + 1) * P],
                                                       tab[b][:, c:c + 1], tab[b][:, CC + c:CC + c + 1],
                                                       ALU.mult, ALU.add)
                    last.then_inc(shifted[b], 1)
                    vec.wait_ge(up[b], 2 * i + 1)
                    for f in range(4):
                        last = nc.vector.tensor_scalar(h[b][:, f, :], ps_h[b][:, 0, f * P:(f + 1) * P],
                                                       tab[b][:, 2 * CC + f:2 * CC + f + 1], 0.0, ALU.add, ALU.max)
                    last.then_inc(relu_v[b], 1)
                    vec.wait_ge(down[b], i + 2)
                    vec.wait_ge(stored[b], 16 * (i + 1))
                    nc.vector.tensor_copy(y[b][:, :], ps_y[:, b, :]).then_inc(copied[b], 1)

        @block.scalar
        def _(act):
            for b in range(B):
                act.sem_inc(stored[b], 16)
            with act.Fori(0, steps) as i:
                for b in range(B):
                    act.wait_ge(up[b], 2 * i + 2)
                    for f in range(4, FC):
                        last = nc.scalar.activation(h[b][:, f, :], ps_h[b][:, 1, (f - 4) * P:(f - 3) * P], ACT.Relu,
                                                    bias=tab[b][:, 2 * CC + f:2 * CC + f + 1])
                    last.then_inc(relu_a[b], 1)
                    act.wait_ge(copied[b], i + 2)
                    act.dma_start(d["sorted_y"][bass.ds((i * B + b) * P, P), :], y[b][:, :]).then_inc(stored[b], 16)
            for b in range(B):
                act.wait_ge(stored[b], 16 * (steps + 1))
    t.ctx.close()


def l0_combine(nc, mem, d, m):
    t = Memory(nc, mem.sems)
    H = NT // 2
    got = t.sb("got", [P, H, C])
    X = t.sb("Xr", [P, H, C])
    y_in, x_in = mem.sem("y_gathered"), mem.sem("x_again")
    given, gated, out = mem.sem("silu_in"), mem.sem("silu_out"), mem.sem("x1_made")
    stored = mem.sem("x1_stored")
    chain = mem.sem("combine_chain")
    x_t = d["x"].rearrange("(t p) c -> p t c", p=P)
    x1_t = d["x1"].rearrange("(t p) c -> p t c", p=P)
    with nc.Block() as block:
        @block.gpsimd
        def _(pool):
            for k in range(2):
                if k:
                    pool.wait_ge(out, 1)
                    pool.wait_ge(stored, 16)
                for i in range(H):
                    nc.gpsimd.indirect_dma_start(
                        out=got[:, i, :], out_offset=None, in_=d["sorted_y"],
                        in_offset=bass.IndirectOffsetOnAxis(ap=m.place[:, k * H + i:k * H + i + 1], axis=0)
                    ).then_inc(y_in, 16)

        @block.sync
        def _(sp):
            for k in range(2):
                if k:
                    sp.wait_ge(stored, 16)
                sp.dma_start(X[:, :, :], x_t[:, k * H:(k + 1) * H, :]).then_inc(x_in, 16)
                sp.wait_ge(out, k + 1)
                sp.dma_start(x1_t[:, k * H:(k + 1) * H, :], X[:, :, :]).then_inc(stored, 16)
            sp.wait_ge(stored, 32)

        @block.vector
        def _(vec):
            ch = Chain(vec, chain)
            for k in range(2):
                vec.wait_ge(y_in, 16 * H * (k + 1))
                for i in range(H):
                    g = k * H + i
                    last = nc.vector.scalar_tensor_tensor(got[:, i, :], got[:, i, :], m.sig[:, g:g + 1],
                                                          m.xn[:, g, :], ALU.mult, ALU.add)
                last.then_inc(given, 1)
                vec.wait_ge(gated, k + 1)
                for i in range(H):
                    g = k * H + i
                    last = nc.vector.scalar_tensor_tensor(got[:, i, :], m.agv[:, :], m.tok[:, g:g + 1],
                                                          got[:, i, :], ALU.mult, ALU.mult)
                ch.link(last)
                vec.wait_ge(x_in, 16 * (k + 1))
                nc.vector.tensor_tensor(X[:, :, :], X[:, :, :], got[:, :, :], ALU.add).then_inc(out, 1)

        @block.scalar
        def _(act):
            for k in range(2):
                act.wait_ge(given, k + 1)
                nc.scalar.activation(got[:, :, :], got[:, :, :], ACT.Silu).then_inc(gated, 1)
    t.ctx.close()


H = 16
HD = C // H
PAIRS = H // 2
QB = 512
NQ = N // QB
QT = QB // P
GK = 2
ROWS = 64
SPEC = 32
NSPEC = 6
LO = SPEC + NSPEC
MASKED = -1e30
MSCALE = 256.0
GROUPS = sum(GK * (q + 1) for q in range(NQ))
SLOTS = 2 * GROUPS
CHUNKS = sum(2 * QT * (q + 1) for q in range(NQ))
AHEAD = 2 * QT * NQ + 12
LEAD = 7


class Count:

    def __init__(self, mem, name, per, credit=0):
        self.sem, self.per, self.credit = mem.sem(name), per, credit

    def at(self, i, k):
        return i * self.per + (self.credit + k)


def l1_normalise(nc, mem, d, m):
    t = Memory(nc, mem.sems)
    X = t.sb("X1", [P, NT, C])
    stats, mv = t.sb("stats1", [P, NT, 6]), t.sb("mv1", [P, NT, 2])
    sd, rstd, sq = t.sb("sd1", [P, NT]), t.sb("rstd1", [P, NT]), t.sb("sq1", [P, NT])
    x_in, given, rooted = mem.sem("x1_in"), mem.sem("stats1_given"), mem.sem("dev1_given")
    chain = mem.sem("l1_norm_chain")
    with nc.Block() as block:
        @block.sync
        def _(sp):
            sp.dma_start(X[:, :, :], d["x1"].rearrange("(t p) c -> p t c", p=P)).then_inc(x_in, 16)

        @block.vector
        def _(vec):
            ch = Chain(vec, chain)
            vec.wait_ge(x_in, 16)
            row_statistics(nc, vec, ch, X, stats, mv, given)
            vec.wait_ge(rooted, 1)
            ch.link(nc.vector.reciprocal(rstd[:, :], sd[:, :]))
            apply_statistics(nc, vec, ch, X, m.xn, mv, rstd)
            row_statistics(nc, vec, ch, m.xn, stats, mv, given)
            vec.wait_ge(given, 2 * NT)
            ch.link(nc.vector.tensor_tensor(sq[:, :], mv[:, :, 0], mv[:, :, 0], ALU.mult))
            nc.vector.tensor_tensor(sq[:, :], sq[:, :], mv[:, :, 1], ALU.add).then_inc(given, 1)
            vec.wait_ge(rooted, 2)
            ch.link(nc.vector.tensor_scalar(sd[:, :], sd[:, :], 1e-12, None, ALU.max))
            ch.link(nc.vector.reciprocal(rstd[:, :], sd[:, :]))
            with vec.Fori(0, NT) as i:
                nc.vector.tensor_scalar(m.xg[:, bass.ds(i, 1), :], m.xn[:, bass.ds(i, 1), :],
                                        rstd[:, bass.ds(i, 1)], float(C) ** 0.5, ALU.mult, ALU.mult
                                        ).then_inc(ch.sem, 1)
            ch.n += NT
            vec.wait_ge(ch.sem, ch.n)

        @block.scalar
        def _(act):
            act.wait_ge(given, NT)
            nc.scalar.activation(sd[:, :], mv[:, :, 1], ACT.Sqrt, bias=m.eps[:, :]).then_inc(rooted, 1)
            act.wait_ge(given, 2 * NT + 1)
            nc.scalar.activation(sd[:, :], sq[:, :], ACT.Sqrt, scale=float(C)).then_inc(rooted, 1)
    t.ctx.close()


def l1_gain(nc, mem, d, m, xgT):
    gamma = m.gamma
    g_in, scaled, kept = mem.sem("gamma_in"), mem.sem("gamma_applied"), mem.sem("xg_kept")
    with nc.Block() as block:
        @block.sync
        def _(sp):
            sp.dma_start(gamma[:, :], d["gamma"]).then_inc(g_in, 16)
            for c in range(CC):
                sp.wait_ge(scaled, c + 1)
                sp.dma_start(d["xgT"][:, c, :], xgT[:, c, :]).then_inc(kept, 16)
            sp.wait_ge(kept, 16 * CC)

        @block.vector
        def _(vec):
            vec.wait_ge(g_in, 16)
            for c in range(CC):
                nc.vector.tensor_scalar(xgT[:, c, :], xgT[:, c, :], gamma[:, c:c + 1], None,
                                        ALU.mult).then_inc(scaled, 1)


def l1_values(nc, mem, d, m):
    t = Memory(nc, mem.sems)
    wv, bv = t.sb("wv", [P, CC, C]), t.sb("bv", [P, C])
    wkq, bkq = t.sb("wkq", [P, 2, CC, C]), t.sb("bkq", [P, 2, CC])
    x32 = [t.sb(f"x32_{b}", [P, QB]) for b in range(2)]
    BATCH = NQ // 2
    halves = [t.sb(f"halves{b}", [P, 2, BATCH * QB], F16) for b in range(2)]
    ps = [t.ps(f"ps_v{b}", [P, 2, C]) for b in range(4)]
    ps_kq = [t.ps(f"ps_kq{b}", [P, QB]) for b in range(4)]
    w_in, summed, added = mem.sem("wv_in"), mem.sem("v_summed"), mem.sem("v_added")
    scaled, projected, biased = mem.sem("query_bias_scaled"), mem.sem("kq_projected"), mem.sem("kq_biased")
    high, split = mem.sem("kq_high_given"), mem.sem("kq_split")
    kept = [mem.sem(f"kq_kept{b}") for b in range(2)]
    steps = [(w, c, q) for w in range(2) for c in range(CC) for q in range(NQ)]
    with nc.Block() as block:
        @block.sync
        def _(sp):
            sp.dma_start(wv[:, :, :], d["wv"].rearrange("(k p) c -> p k c", p=P)).then_inc(w_in, 16)
            sp.dma_start(bv[:, :], d["bv"].broadcast_to([P, C])).then_inc(w_in, 16)
            for w in range(2):
                sp.dma_start(wkq[:, w, :, :], d["wkq"][w].rearrange("(k p) c -> p k c", p=P)).then_inc(w_in, 16)
            sp.dma_start(bkq[:, :, :], d["bkq"]).then_inc(w_in, 16)
            for dst, src in m.attn_loads:
                sp.dma_start(dst, src).then_inc(w_in, 16)
            for n in range(0, len(steps), BATCH):
                w, c, q = steps[n]
                b = n // BATCH % 2
                sp.wait_ge(split, n + BATCH)
                sp.dma_start(d["kq16"][w, :, c * P:(c + 1) * P, q * QB:(q + BATCH) * QB].rearrange("s r n -> r s n"),
                             halves[b][:, :, :]).then_inc(kept[b], 16)
            sp.wait_ge(w_in, 16 * (5 + len(m.attn_loads)))
            for b in range(2):
                sp.wait_ge(kept[b], 16 * len(steps) // BATCH // 2)

        @block.gpsimd
        def _(pool):
            parts = [(m.vall[:, :, :, HD:HD + 1], 1.0), (m.stage[:, :, :], 0.0), (m.identb[:, :], 0.0),
                     (m.after[:, :], 0.0), (m.before[:, :], 0.0)]
            for u in range(2):
                parts += [(m.vpair[u][:, :, :, HD:], 0.0), (m.ka[u][:, :], 0.0),
                          (m.qa[u][0][:, :], 0.0), (m.qa[u][1][:, :], 0.0)]
            for k, (part, value) in enumerate(parts):
                nc.gpsimd.memset(part, value).then_inc(added, 1)
                pool.wait_ge(added, k + 1)
            for mask, op, fill, base, step in ((m.identb, ALU.not_equal, 1.0, 0, -1), (m.after, ALU.is_ge, MASKED, 0, -1),
                                               (m.before, ALU.is_ge, MASKED, P - QB, 1)):
                nc.gpsimd.affine_select(out=mask[:, :], in_=mask[:, :], compare_op=op, fill=fill, base=base,
                                        pattern=[[step, mask.shape[1]]], channel_multiplier=-step).then_inc(added, 1)

        @block.tensor
        def _(pe):
            pe.wait_ge(w_in, 16 * (5 + len(m.attn_loads)))
            for g in range(NT // 2):
                if g >= 4:
                    pe.wait_ge(m.v_free, g - 3)
                for j in range(2):
                    i = 2 * g + j
                    for c in range(CC):
                        last = nc.tensor.matmul(ps[g % 4][:, j, :], m.xnT[:, c, i * P:(i + 1) * P], wv[:, c, :],
                                                start=(c == 0), stop=(c == CC - 1))
                last.then_inc(summed, 1)
            for n, (w, c, q) in enumerate(steps):
                if n >= 4:
                    pe.wait_ge(biased, n - 3)
                for k in range(CC):
                    last = nc.tensor.matmul(ps_kq[n % 4][:, :], wkq[:, w, k, c * P:(c + 1) * P],
                                            m.xnT[:, k, q * QB:(q + 1) * QB], start=(k == 0), stop=(k == CC - 1))
                last.then_inc(projected, 1)

        @block.scalar
        def _(act):
            act.wait_ge(scaled, 1)
            for n, (w, c, q) in enumerate(steps):
                act.wait_ge(projected, n + 1)
                if n >= 2:
                    act.wait_ge(split, n - 1)
                nc.scalar.activation(x32[n % 2][:, :], ps_kq[n % 4][:, :], ACT.Identity, bias=bkq[:, w, c:c + 1],
                                     scale=(float(HD) ** -0.5 if w else 1.0)).then_inc(biased, 1)

        @block.vector
        def _(vec):
            vec.wait_ge(w_in, 16 * (5 + len(m.attn_loads)))
            nc.vector.tensor_scalar(bkq[:, 1, :], bkq[:, 1, :], float(HD) ** -0.5, None, ALU.mult).then_inc(scaled, 1)
            for g in range(NT // 2):
                vec.wait_ge(summed, g + 1)
                nc.vector.tensor_tensor(
                    m.vall[:, 2 * g:2 * g + 2, :, 0:HD],
                    ps[g % 4][:, :, :].rearrange("p j (h e) -> p j h e", h=H),
                    bv[:, :].rearrange("p (h e) -> p h e", h=H).unsqueeze(1).broadcast_to([P, 2, H, HD]),
                    ALU.add).then_inc(m.v_free, 1)
            for n, (w, c, q) in enumerate(steps):
                b = n // BATCH % 2
                hold = halves[b]
                cols = slice(q % BATCH * QB, (q % BATCH + 1) * QB)
                vec.wait_ge(biased, n + 1)
                if n % BATCH == 0 and n >= 2 * BATCH:
                    vec.wait_ge(kept[b], 16 * (n // BATCH // 2))
                nc.vector.tensor_copy(hold[:, 0, cols], x32[n % 2][:, :]).then_inc(high, 1)
                vec.wait_ge(high, n + 1)
                nc.vector.tensor_tensor(hold[:, 1, cols], x32[n % 2][:, :], hold[:, 0, cols],
                                        ALU.subtract).then_inc(split, 1)
    t.ctx.close()


def l1_attention(nc, mem, d, m):
    t = Memory(nc, mem.sems)
    pT = [t.sb(f"pT{b}", [P, GK, QB]) for b in range(4)]
    o_sb = t.sb("o_sb", [P, QB])
    mxc = t.sb("mxc", [P, 2, QT, NQ])
    mx = t.sb("mx", [P, 2, QT])
    rden = t.sb("rden", [P, QT, 2])
    abias = [t.sb(f"abias_pair{u}", [P, 2, GK * NQ]) for u in range(2)]
    gates = mem.sem("attention_gates")
    st = t.ps("st", [P, 2, GK, QB])
    sq = t.ps("sq", [P, 2, QB])
    o4 = t.ps("o4", [P, QB])
    misc = t.ps("misc", [P, 512])
    turned = misc[:, 0:256].bitcast(F16).rearrange("p (a q) -> p a q", a=QT)
    picked = misc[:, 256:256 + QT * 2 * (HD + 1)].rearrange("p (a h e) -> p a h e", a=QT, h=2)
    LOADS = 16
    c_load = [Count(mem, f"pair{u}_loaded", 16 * LOADS) for u in range(2)]
    c_vp = Count(mem, "pair_values_copied", 2)
    c_sq = Count(mem, "scores_for_maxima", CHUNKS)
    c_max = Count(mem, "maxima_taken", CHUNKS, 2)
    c_stage = Count(mem, "maxima_staged", NQ)
    c_turn = Count(mem, "maxima_transposed", NQ)
    c_rows = Count(mem, "maxima_rows_in", NQ)
    c_st = Count(mem, "scores_ready", SLOTS)
    c_exp = Count(mem, "exponentials_ready", SLOTS, 2)
    c_pv = Count(mem, "exponentials_used", GROUPS, GROUPS + 2)
    c_osb = Count(mem, "block_copied", NQ, 1)
    c_pick = Count(mem, "block_picked", NQ)
    c_att = Count(mem, "block_normalised", NQ, 1)
    chain = mem.sem("attention_chain")

    chunks = [(b, hd, a, k) for b in range(NQ) for hd in range(2) for a in range(QT) for k in range(b + 1)]
    slots = [(b, g, hd) for b in range(NQ) for g in range(GK * (b + 1)) for hd in range(2)]
    first_slot = {b: slots.index((b, 0, 0)) for b in range(NQ)}
    chunks_end = [2 * QT * (b + 1) * (b + 2) // 2 for b in range(NQ)]

    def where(p, u, s, length):
        return (p, u, s) if s < length else (p + 1, 1 - u, s - length)

    def turn_slot(b, nxt):
        return (chunks_end[b] + nxt * CHUNKS - AHEAD + 1) // 2 + 2

    def turn_at(s):
        for b in range(NQ):
            for nxt in range(2):
                if turn_slot(b, nxt) == s:
                    return b, nxt
        return None

    def turns_until(s):
        return sum(turn_slot(b, nxt) <= s for b in range(NQ) for nxt in range(2))

    def picks_before(s):
        return sum(first_slot[b] + PICK < s for b in range(NQ)) - 1

    COPY, PICK = 2, 6
    def block_before(s, lag):
        for b, s0 in first_slot.items():
            if s0 + lag == s:
                return (b - 1) % NQ, b == 0
        return None

    with nc.Block() as block:
        @block.sync
        def _(sp):
            def load(p, u, source):
                sp.wait_ge(c_pv.sem, c_pv.at(p, -GROUPS))
                ka, qa = m.ka[u], m.qa[u]
                for hd in range(2):
                    r0 = hd * ROWS
                    h = bass.ds(2 * source + hd, 1)
                    for which, dst, order in ((0, ka, (0, 1, 0)), (1, qa[hd], (0, 0, 1))):
                        for half, r in zip(order, (0, HD, LO)):
                            sp.dma_start(dst[r0 + r:r0 + r + HD, :], heads[which, half, h, :, :]
                                         ).then_inc(c_load[u].sem, 16)
                    sp.dma_start(ka[r0 + SPEC:r0 + LO, :], d["kspec"][h, :, :]).then_inc(c_load[u].sem, 16)
                    sp.dma_start(qa[hd][r0 + SPEC:r0 + LO, :], d["qspec"]).then_inc(c_load[u].sem, 16)

            heads = d["kq16"].rearrange("w s (h e) n -> w s h e n", e=HD)
            with sp.Fori(0, PAIRS // 2) as i:
                for u in range(2):
                    load(2 * i + u, u, 2 * i + u)
            load(PAIRS, 0, 0)
            sp.wait_ge(c_load[0].sem, c_load[0].at(PAIRS // 2, 16 * LOADS))

        @block.gpsimd
        def _(pool):
            def prepare(p, u, source):
                pool.wait_ge(c_pv.sem, c_pv.at(p, -GROUPS))
                pool.sem_inc(gates, 1)
                nc.gpsimd.tensor_copy(m.vpair[u][:, :, :, 0:HD + 1],
                                      m.vall[:, :, bass.ds(2 * source, 2), :]).then_inc(c_vp.sem, 1)
                nc.gpsimd.tensor_copy(abias[u][:, :, :], m.abias[:, bass.ds(2 * source, 2), :]).then_inc(c_vp.sem, 1)

            with pool.Fori(0, PAIRS // 2) as i:
                for u in range(2):
                    prepare(2 * i + u, u, 2 * i + u)
            prepare(PAIRS, 0, 0)

        @block.scalar
        def _(act):
            def exponential(p, u, s):
                b, g, hd = slots[s]
                q0 = QB // 2 if g == GK * b + 1 else 0
                if s == 0:
                    act.wait_ge(c_vp.sem, c_vp.at(p, c_vp.per))
                act.wait_ge(c_st.sem, c_st.at(p, s + 1))
                act.wait_ge(c_pv.sem, c_pv.at(p, s // 2 - 1))
                kt = g - GK * b + GK * (NQ - 1)
                nc.scalar.activation(pT[s % 4][:, :, q0:], st[:, s % 2, :, q0:], ACT.Exp,
                                     bias=abias[u][:, hd, kt:kt + 1]).then_inc(c_exp.sem, 1)

            def take_rows(p, u, b):
                act.wait_ge(c_turn.sem, c_turn.at(p, b + 1))
                for hd in range(2):
                    r = hd * ROWS + SPEC
                    last = nc.scalar.copy(
                        m.qa[u][hd][r:r + NSPEC, b * QB:(b + 1) * QB].rearrange("p (a q) -> p a q", a=QT),
                        turned[r:r + NSPEC, :, :])
                last.then_inc(c_rows.sem, 1)

            def copy_block(p, b):
                act.wait_ge(c_pv.sem, c_pv.at(p, GK * (b + 1) * (b + 2) // 2))
                act.wait_ge(c_pick.sem, c_pick.at(p, b))
                nc.scalar.copy(o_sb[:, :], o4[:, :]).then_inc(c_osb.sem, 1)

            def slot(p, u, s, began=True):
                p, u, s = where(p, u, s, SLOTS)
                exponential(p, u, s)
                turn = turn_at(s)
                if turn:
                    b, nxt = turn
                    take_rows(p + nxt, u ^ nxt, b)
                done = block_before(s, COPY)
                if done and (began or not done[1]):
                    copy_block(p - 1 if done[1] else p, done[0])

            act.sem_inc(c_exp.sem, c_exp.credit)
            act.sem_inc(c_osb.sem, c_osb.credit)
            for b in range(NQ):
                if chunks_end[b] <= AHEAD:
                    take_rows(0, 0, b)
            for s in range(LEAD):
                slot(0, 0, s, began=False)
            with act.Fori(0, PAIRS // 2) as i:
                for u in range(2):
                    for s in range(LEAD, LEAD + SLOTS):
                        slot(2 * i + u, u, s)

        @block.vector
        def _(vec):
            ch = Chain(vec, chain)

            def stage_maxima(p, b):
                vec.wait_ge(c_max.sem, c_max.at(p, chunks_end[b]))
                ch.link(nc.vector.tensor_reduce(mx[:, :, :], mxc[:, :, :, 0:b + 1], AXX, ALU.max))
                for hd in range(2):
                    last = nc.vector.tensor_scalar(mx[:, hd, :], mx[:, hd, :], -1.0 / MSCALE,
                                                   m.start[:, bass.ds(2 * p + hd, 1), b], ALU.mult, ALU.add)
                ch.link(last)
                vec.wait_ge(c_turn.sem, c_turn.at(p, b))
                if b == 0:
                    for hd in range(2):
                        last = nc.vector.tensor_copy(
                            m.stage[:, :, hd * ROWS + SPEC + 2:hd * ROWS + SPEC + 4],
                            m.slopes[:, bass.ds(2 * p + hd, 1), :].broadcast_to([P, QT, 2]))
                    ch.link(last)
                hi = m.stage[:, :, :].rearrange("p a (h r) -> p h a r", h=2)
                ch.link(nc.vector.tensor_copy(hi[:, :, :, SPEC], mx[:, :, :]))
                nc.vector.tensor_tensor(hi[:, :, :, SPEC + 1], mx[:, :, :], hi[:, :, :, SPEC],
                                        ALU.subtract).then_inc(c_stage.sem, 1)

            def maxima(p, lo, hi):
                for x in range(lo, hi):
                    pp, _, n = where(p, 0, x, CHUNKS)
                    b, hd, a, k = chunks[n]
                    w = (a + 1) * P if k == b else QB
                    vec.wait_ge(c_sq.sem, c_sq.at(pp, n + 1))
                    nc.vector.tensor_reduce(mxc[:, hd, a, k:k + 1], sq[:, n % 2, 0:w], AXX,
                                            ALU.max).then_inc(c_max.sem, 1)
                    if n + 1 == chunks_end[b]:
                        stage_maxima(pp, b)

            def normalise(p, b):
                vec.wait_ge(c_pick.sem, c_pick.at(p, b + 1))
                ch.link(nc.vector.reciprocal(rden[:, :, :], picked[:, :, :, HD]))
                nc.vector.tensor_tensor(
                    m.att[:, b * QT:(b + 1) * QT, bass.ds(2 * HD * p, 2 * HD)].rearrange("p a (h e) -> p a h e", h=2),
                    picked[:, :, :, 0:HD], rden[:, :, :].unsqueeze(3).broadcast_to([P, QT, 2, HD]),
                    ALU.mult).then_inc(c_att.sem, 1)

            def slot(p, s, began=True):
                p, _, s = where(p, 0, s, SLOTS)
                maxima(p, AHEAD + 2 * s, AHEAD + 2 * s + 2)
                done = block_before(s, PICK)
                if done and (began or not done[1]):
                    normalise(p - 1 if done[1] else p, done[0])

            vec.sem_inc(c_max.sem, c_max.credit)
            vec.sem_inc(c_att.sem, c_att.credit)
            maxima(0, 0, AHEAD)
            for s in range(LEAD):
                slot(0, s, began=False)
            with vec.Fori(0, PAIRS // 2) as i:
                ch.enter(i, 2 * (4 * NQ + 1))
                for u in range(2):
                    for s in range(LEAD, LEAD + SLOTS):
                        slot(2 * i + u, s)
                ch.leave(PAIRS // 2)

        @block.tensor
        def _(pe):
            mm = nc.tensor.matmul

            def maxima_scores(i, u, lo, hi):
                for x in range(lo, hi):
                    p, uu, n = where(2 * i + u, u, x, CHUNKS)
                    b, hd, a, k = chunks[n]
                    w = (a + 1) * P if k == b else QB
                    if n == 0:
                        pe.wait_ge(c_load[uu].sem, c_load[uu].at(i, 16 * LOADS * (2 if uu < u else 1)))
                    pe.wait_ge(c_max.sem, c_max.at(p, n - 1))
                    q = b * QB + a * P
                    last = mm(sq[:, n % 2, 0:w], m.qa[uu][hd][:, q:q + P], m.ka[uu][:, k * QB:k * QB + w],
                              start=True, stop=(k < b))
                    if k == b:
                        last = mm(sq[:, n % 2, a * P:w], m.identb[:, :], m.after[:, :], start=False, stop=True)
                    last.then_inc(c_sq.sem, 1)

            def scores(p, u, s):
                b, g, hd = slots[s]
                q0 = QB // 2 if g == GK * b + 1 else 0
                if g == 0 and hd == 0:
                    pe.wait_ge(c_rows.sem, c_rows.at(p, b + 1))
                pe.wait_ge(c_exp.sem, c_exp.at(p, s - 1))
                for j in range(GK):
                    kt = GK * g + j
                    r = kt - QT * b
                    last = mm(st[:, s % 2, j, q0:], m.ka[u][:, kt * P:(kt + 1) * P],
                              m.qa[u][hd][:, b * QB + q0:(b + 1) * QB], start=True, stop=(r < 0))
                    if r >= 0:
                        w = (r + 1) * P - q0
                        last = mm(st[:, s % 2, j, q0:q0 + w], m.identb[:, :], m.before[:, QB - w:],
                                  start=False, stop=True)
                last.then_inc(c_st.sem, 1)

            def weighted(p, u, s):
                b, g, _ = slots[s]
                q0 = QB // 2 if g == GK * b + 1 else 0
                pe.wait_ge(c_exp.sem, c_exp.at(p, s + 2))
                if g == 0:
                    if b == 0:
                        pe.wait_ge(c_vp.sem, c_vp.at(p, c_vp.per))
                    pe.wait_ge(c_osb.sem, c_osb.at(p, b))
                for hd in range(2):
                    for j in range(GK):
                        r = (GK * hd + j) * 32
                        last = mm(o4[r:r + 32, q0:], m.vpair[u][:, GK * g + j, hd, :], pT[(s + hd) % 4][:, j, q0:],
                                  start=(g == 0), stop=(g == GK * b + 1))
                last.then_inc(c_pv.sem, 1)

            def turn(p, b):
                pe.wait_ge(c_rows.sem, c_rows.at(p, b))
                pe.wait_ge(c_stage.sem, c_stage.at(p, b + 1))
                for a in range(QT):
                    last = nc.tensor.transpose(turned[:, a, :], m.stage[:, a, :], m.ident16[:, :])
                last.then_inc(c_turn.sem, 1)

            def pick(p, b, rows):
                pe.wait_ge(c_osb.sem, c_osb.at(p, b + 1))
                pe.wait_ge(c_att.sem, c_att.at(p, b))
                pe.wait_ge(c_rows.sem, rows)
                for a in range(QT):
                    last = mm(misc[:, 256 + a * 2 * (HD + 1):256 + (a + 1) * 2 * (HD + 1)],
                              o_sb[:, a * P:(a + 1) * P], m.pick[:, :], start=True, stop=True)
                last.then_inc(c_pick.sem, 1)

            def slot(i, u, s, began=True):
                p, uu, n = where(2 * i + u, u, s, SLOTS)
                x = AHEAD + 2 * s
                if n % 2 == 0:
                    maxima_scores(i, u, x, x + 1)
                scores(p, uu, n)
                turned_now = turn_at(n)
                if turned_now:
                    pe.wait_ge(c_att.sem, c_att.at(p, picks_before(n)))
                    turn(p + turned_now[1], turned_now[0])
                maxima_scores(i, u, x + 1 - n % 2, x + 2)
                if n % 2 == 1:
                    if n >= 2:
                        weighted(p, uu, n - 3)
                    elif began:
                        weighted(p - 1, 1 - uu, n - 3 + SLOTS)
                done = block_before(n, PICK)
                if done and (began or not done[1]):
                    pick(p - 1 if done[1] else p, done[0], c_rows.at(p, turns_until(n)))

            pe.sem_inc(c_pv.sem, c_pv.credit)
            for b in range(NQ):
                if chunks_end[b] <= AHEAD:
                    maxima_scores(0, 0, chunks_end[b - 1] if b else 0, chunks_end[b])
                    turn(0, b)
                    rest_from = chunks_end[b]
            maxima_scores(0, 0, rest_from, AHEAD)
            for s in range(LEAD):
                slot(0, 0, s, began=False)
            with pe.Fori(0, PAIRS // 2) as i:
                for u in range(2):
                    for s in range(LEAD, LEAD + SLOTS):
                        slot(i, u, s)
    t.ctx.close()


def l1_output(nc, mem, d, m, attT):
    t = Memory(nc, mem.sems)
    wo, bo = t.sb("wo", [P, CC, C]), t.sb("bo", [P, C])
    s = [t.sb(f"s_sb{b}", [P, 4, C]) for b in range(2)]
    ps = [t.ps(f"ps_o{b}", [P, 4, C]) for b in range(2)]
    w_in, summed, added = mem.sem("wo_in"), mem.sem("o_summed"), mem.sem("o_added")
    kept = [mem.sem(f"s_kept{b}") for b in range(2)]
    s_t = d["s1"].rearrange("(t p) c -> p t c", p=P)
    with nc.Block() as block:
        @block.sync
        def _(sp):
            sp.dma_start(wo[:, :, :], d["wo"].rearrange("(k p) c -> p k c", p=P)).then_inc(w_in, 16)
            sp.dma_start(bo[:, :], d["bo"].broadcast_to([P, C])).then_inc(w_in, 16)
            for g in range(NT // 4):
                sp.wait_ge(added, g + 1)
                sp.dma_start(s_t[:, 4 * g:4 * g + 4, :], s[g % 2][:, :, :]).then_inc(kept[g % 2], 16)
            for b in range(2):
                sp.wait_ge(kept[b], 16 * (NT // 8))

        @block.tensor
        def _(pe):
            pe.wait_ge(w_in, 32)
            for g in range(NT // 4):
                if g >= 2:
                    pe.wait_ge(added, g - 1)
                for j in range(4):
                    i = 4 * g + j
                    for c in range(CC):
                        last = nc.tensor.matmul(ps[g % 2][:, j, :], attT[:, c, i * P:(i + 1) * P], wo[:, c, :],
                                                start=(c == 0), stop=(c == CC - 1))
                last.then_inc(summed, 1)

        @block.vector
        def _(vec):
            vec.wait_ge(w_in, 32)
            for g in range(NT // 4):
                vec.wait_ge(summed, g + 1)
                if g >= 2:
                    vec.wait_ge(kept[g % 2], 16 * (g // 2))
                nc.vector.tensor_tensor(s[g % 2][:, :, :], ps[g % 2][:, :, :],
                                        bo[:, :].unsqueeze(1).broadcast_to([P, 4, C]), ALU.add).then_inc(added, 1)
    t.ctx.close()


def layer1(nc, mem, sems, d, m):
    a = Memory(nc, sems)
    m.xnT = a.sb("xn1T", [P, CC, N])
    m.gamma = a.sb("gamma", [P, CC])
    b = Memory(nc, sems)
    m.xn, m.xg = b.sb("xn1", [P, NT, C]), b.sb("xg", [P, NT, C])
    l1_normalise(nc, mem, d, m)
    transpose_rows(nc, mem, "xg", m.ident, m.xg, m.xnT)
    l1_gain(nc, mem, d, m, m.xnT)
    transpose_rows(nc, mem, "xn1", m.ident, m.xn, m.xnT)
    b.ctx.close()
    b = Memory(nc, sems)
    m.att = b.sb("att", [P, NT, C])
    c = Memory(nc, sems)
    m.vall = c.sb("vall", [P, NT, H, HD + 1])
    m.vpair = [c.sb(f"vpair{u}", [P, NT, 2, 32]) for u in range(2)]
    m.ka = [c.sb(f"ka{u}", [P, N], F16) for u in range(2)]
    m.qa = [[c.sb(f"qa{u}_{h}", [P, N], F16) for h in range(2)] for u in range(2)]
    m.stage = c.sb("stage", [P, QT, P], F16)
    m.slopes = c.sb("slopes", [P, H + 2, 2], F16)
    m.start = c.sb("start", [P, H + 2, NQ])
    m.abias = c.sb("abias", [P, H, GK * NQ])
    m.ident16, m.identb = c.sb("ident16", [P, P], F16), c.sb("identb", [P, P], BF16)
    m.after, m.before = c.sb("after", [P, P], BF16), c.sb("before", [P, QB], BF16)
    m.pick = c.sb("pick", [P, 2 * (HD + 1)])
    m.v_free = mem.sem("v_bank_free")
    m.attn_loads = [(m.slopes[:, :, :], d["slopes"]), (m.start[:, :, :], d["start"]), (m.abias[:, :, :], d["abias"]),
                    (m.ident16[:, :], d["ident16"]), (m.pick[:, :], d["pick"])]
    l1_values(nc, mem, d, m)
    l1_attention(nc, mem, d, m)
    c.ctx.close()
    transpose_rows(nc, mem, "att", m.ident, m.att, m.xnT)
    l1_output(nc, mem, d, m, m.xnT)
    b.ctx.close()
    a.ctx.close()




PH = 8
KEYS = 64
TOP = 16
TABLE_ROWS = KEYS * KEYS
JJ = 32
RUNS = [(a, TOP // (a + 1)) for a in range(TOP)]
CAND = sum(n for _, n in RUNS)
FIRST = [sum(n for _, n in RUNS[:a]) for a in range(TOP)]
LOWEST = -3.0e38
HB = 4
PB = 16


def lookup_weights(nc, mem, d, m):
    t = Memory(nc, mem.sems)
    wq = t.sb("wq", [P, 2 * PH, C])
    keys = t.sb("keys", [P, 2 * PH, KEYS])
    ps = [t.ps(f"ps_wk{c}", [P, 2 * PH * KEYS]) for c in range(CC)]
    w_in, done, copied = mem.sem("lookup_in"), mem.sem("keys_joined"), mem.sem("keys_copied")
    with nc.Block() as block:
        @block.sync
        def _(sp):
            sp.dma_start(wq[:, :, :], d["pwq"].rearrange("(g p) c -> p g c", p=P)).then_inc(w_in, 16)
            sp.dma_start(keys[:, :, :], d["keysT"]).then_inc(w_in, 16)
            sp.dma_start(m.down[:, :, :, :], d["down"]).then_inc(w_in, 16)
            sp.dma_start(m.up[:, :, :], d["up"]).then_inc(w_in, 16)
            sp.dma_start(m.count[:, :, :], d["count"]).then_inc(w_in, 16)
            sp.dma_start(m.column[:, :, :], d["column"]).then_inc(w_in, 16)
            sp.dma_start(m.shift[:, :], d["shift"]).then_inc(w_in, 16)
            sp.wait_ge(w_in, 16 * 7)

        @block.tensor
        def _(pe):
            pe.wait_ge(w_in, 16 * 7)
            for c in range(CC):
                for g in range(2 * PH):
                    last = nc.tensor.matmul(ps[c][:, g * KEYS:(g + 1) * KEYS], wq[:, g, c * P:(c + 1) * P],
                                            keys[:, g, :], start=True, stop=True)
                last.then_inc(done, 1)

        @block.vector
        def _(vec):
            for c in range(CC):
                vec.wait_ge(done, c + 1)
                nc.vector.tensor_copy(m.wk[:, c, :], ps[c][:, :]).then_inc(copied, 1)
    t.ctx.close()


def lookup_experts(nc, mem, d, m):
    t = Memory(nc, mem.sems)
    xs, xh = t.sb("xs_t", [P, CC, P]), t.sb("xh_t", [P, CC, P])
    S = t.sb("S", [P, 2 * PH, KEYS])
    val, idx = t.sb("val", [P, 2 * PH, TOP]), t.sb("idx", [P, 2 * PH, TOP], U32)
    code = t.sb("code", [P, 2 * PH, TOP])
    over = t.sb("over", [P, PH, TOP])
    cand, left = t.sb("cand", [P, PH, CAND]), t.sb("left", [P, PH, CAND])
    pay = t.sb("pay", [P, PH, CAND])
    best, pos = t.sb("best", [P, PH, TOP]), t.sb("pos", [P, PH, TOP], U32)
    pos16 = t.sb("pos16", [P, PH, TOP], F16)
    hit = t.sb("hit", [P, PH, CAND, TOP], F16)
    sel = t.sb("sel", [P, PH, CAND, TOP])
    e, den = t.sb("e", [P, PH, TOP]), t.sb("den", [P, PH])
    wgt = t.sb("wgt", [P, P])
    coden = t.sb("coden", [P, P], I32)
    code_r, code_c = t.sb("code_r", [P, P], I32), t.sb("code_c", [P, P], I32)
    rowf, colf = t.sb("rowf", [P, P]), t.sb("colf", [P, P])
    rowT, colT = t.sb("rowT", [P, P // JJ, P], F16), t.sb("colT", [P, P], F16)
    wT, whT, wlT = t.sb("wT", [P, P]), t.sb("whT", [P, P], F16), t.sb("wlT", [P, P], F16)
    A = t.sb("A", [P, P, P], F16)
    B = t.sb("B", [P, 2, JJ, P], F16)
    G = t.sb("G", [P, JJ, P])
    o_sb = t.sb("peer_o", [P, C])
    ps_s = t.ps("ps_sims", [P, 2 * PH * KEYS])
    ps_h = [t.ps(f"ps_down{b}", [P, HB, P]) for b in range(2)]
    ps_p = [t.ps(f"ps_pick{b}", [P, PB, JJ]) for b in range(2)]
    ps_o = t.ps("ps_up", [P, 512])
    ps_t = t.ps("ps_turn", [P, 4, P])
    NH, NP = JJ // HB, P // PB
    c_xs, c_xh = Count(mem, "xs_in", 16), Count(mem, "xh_in", 16)
    c_sims = Count(mem, "sims_summed", 1, 1)
    c_S = Count(mem, "sims_copied", 1)
    c_val = Count(mem, "keys_found", 1, 1)
    c_top = Count(mem, "pairs_found", 1, 1)
    c_pay = Count(mem, "rows_looked_up", 1, 1)
    c_e = Count(mem, "weights_exponential", 1)
    c_dec = Count(mem, "choice_decoded", 1, 1)
    c_turn = Count(mem, "choice_transposed", 1)
    c_tc = Count(mem, "choice_copied", 1, 1)
    c_low = Count(mem, "low_weights_in", 1)
    c_high = Count(mem, "high_weights_in", 1)
    c_ab = Count(mem, "one_hots_made", 1)
    c_h = Count(mem, "down_summed", NH)
    c_g = Count(mem, "gelu_done", NH, 2)
    c_p = Count(mem, "weights_spread", NP)
    c_w = Count(mem, "weights_applied", NP, 2)
    c_o = Count(mem, "up_summed", 1, 1)
    c_oc = Count(mem, "up_copied", 1, 1)
    c_k = Count(mem, "up_kept", 16, 16)
    chain, pchain = mem.sem("lookup_chain"), mem.sem("lookup_pool_chain")
    gates, pool_gates = mem.sem("lookup_gate"), mem.sem("lookup_pool_gate")
    peer_t = d["peer"].rearrange("(t p) c -> p t c", p=P)

    def wait(eng, c, i, k):
        v = c.at(i, k)
        if not isinstance(v, int) or v > 0:
            eng.wait_ge(c.sem, v)

    def stages(i, peeled):
        if not peeled:
            return True, True, True, True
        return i < NT, 1 <= i <= NT, i >= 2, i + 1 < NT

    def run(eng, step):
        step(0, True)
        step(1, True)
        with eng.Fori(2, NT - 1) as i:
            step(i, False)
        for i in range(NT - 1, NT + 2):
            step(i, True)

    with nc.Block() as block:
        @block.sync
        def _(sp):
            def load_xs(i):
                wait(sp, c_sims, i - 1, 1)
                sp.dma_start(xs[:, :, :], d["xgT"][:, :, bass.ds(i * P, P)]).then_inc(c_xs.sem, 16)

            def step(i, peeled):
                keys, spread, finish, ahead = stages(i, peeled)
                if finish:
                    wait(sp, c_o, i - 3, 1)
                    sp.dma_start(xh[:, :, :], d["xgT"][:, :, bass.ds((i - 2) * P, P)]).then_inc(c_xh.sem, 16)
                if ahead:
                    load_xs(i + 1)
                if finish:
                    wait(sp, c_oc, i - 2, 1)
                    sp.dma_start(peer_t[:, bass.ds(i - 2, 1), :], o_sb[:, :]).then_inc(c_k.sem, 16)

            sp.sem_inc(c_k.sem, 16)
            load_xs(0)
            run(sp, step)
            wait(sp, c_k, NT, 0)

        @block.tensor
        def _(pe):
            mm = nc.tensor.matmul
            pe.sem_inc(c_sims.sem, 1)
            pe.sem_inc(c_o.sem, 1)

            def sims(i):
                wait(pe, c_xs, i, 16)
                wait(pe, c_S, i - 1, 1)
                for h in range(2):
                    for c in range(CC):
                        last = mm(ps_s[:, h * 512:(h + 1) * 512], xs[:, c, :], m.wk[:, c, h * 512:(h + 1) * 512],
                                  start=(c == 0), stop=(c == CC - 1))
                last.then_inc(c_sims.sem, 1)

            def pick(i, lo, hi):
                for g in range(lo, hi):
                    wait(pe, c_w, i, g - 1)
                    for j in range(PB):
                        k = g * PB + j
                        for half in range(2):
                            last = mm(ps_p[g % 2][:, j, :], A[:, :, k], B[:, half, :, k],
                                      start=(half == 0), stop=(half == 1))
                    last.then_inc(c_p.sem, 1)

            def step(i, peeled):
                keys, spread, finish, ahead = stages(i, peeled)
                if finish:
                    wait(pe, c_xh, i - 2, 16)
                    for g in range(NH):
                        wait(pe, c_g, i - 2, g - 1)
                        for j in range(HB):
                            for c in range(CC):
                                last = mm(ps_h[g % 2][:, j, :], m.down[:, c, g * HB + j, :], xh[:, c, :],
                                          start=(c == 0), stop=(c == CC - 1))
                        last.then_inc(c_h.sem, 1)
                    wait(pe, c_ab, i - 2, 1)
                    wait(pe, c_high, i - 2, 1)
                    pick(i - 2, 0, 2)
                if ahead:
                    sims(i + 1)
                if spread:
                    wait(pe, c_dec, i - 1, 1)
                    wait(pe, c_tc, i - 2, 1)
                    for k, src in enumerate((rowf, colf, wgt)):
                        last = nc.tensor.transpose(ps_t[:, k, :], src[:, :], m.ident[:, :])
                    last.then_inc(c_turn.sem, 1)
                if finish:
                    pick(i - 2, 2, NP)
                if finish:
                    wait(pe, c_w, i - 2, NP)
                    wait(pe, c_oc, i - 3, 1)
                    for j in range(JJ):
                        last = mm(ps_o[:, 0:C], G[:, j, :], m.up[:, j, :], start=(j == 0), stop=(j == JJ - 1))
                    last.then_inc(c_o.sem, 1)

            sims(0)
            run(pe, step)

        @block.scalar
        def _(act):
            act.sem_inc(c_g.sem, c_g.credit)
            act.sem_inc(c_oc.sem, 1)
            act.sem_inc(c_tc.sem, 1)

            def copy_sims(i):
                wait(act, c_sims, i, 1)
                wait(act, c_val, i - 1, 1)
                nc.scalar.copy(S[:, :, :], ps_s[:, :].rearrange("p (g k) -> p g k", k=KEYS)).then_inc(c_S.sem, 1)

            def step(i, peeled):
                keys, spread, finish, ahead = stages(i, peeled)
                if finish:
                    wait(act, c_o, i - 3, 1)
                    for g in range(NH):
                        wait(act, c_h, i - 2, g + 1)
                        nc.scalar.activation(G[:, g * HB:(g + 1) * HB, :], ps_h[g % 2][:, :, :],
                                             ACT.Gelu).then_inc(c_g.sem, 1)
                if ahead:
                    copy_sims(i + 1)
                if keys:
                    wait(act, c_top, i, 1)
                    nc.scalar.activation(e[:, :, :], e[:, :, :], ACT.Exp).then_inc(c_e.sem, 1)
                if spread:
                    wait(act, c_turn, i - 1, 1)
                    for k in range(P // JJ):
                        nc.scalar.activation(rowT[:, k, :], ps_t[:, 0, :], ACT.Identity, bias=m.shift[:, k:k + 1])
                    nc.scalar.copy(colT[:, :], ps_t[:, 1, :])
                    nc.scalar.copy(wT[:, :], ps_t[:, 2, :])
                    nc.scalar.copy(whT[:, :], ps_t[:, 2, :]).then_inc(c_tc.sem, 1)
                if finish:
                    wait(act, c_o, i - 2, 1)
                    wait(act, c_k, i - 2, 0)
                    nc.scalar.copy(o_sb[:, :], ps_o[:, 0:C]).then_inc(c_oc.sem, 1)

            copy_sims(0)
            run(act, step)

        @block.gpsimd
        def _(pool):
            pool.sem_inc(c_pay.sem, 1)
            ch = Chain(pool, pchain)
            PER = 9

            def step(i, peeled):
                keys, spread, finish, ahead = stages(i, peeled)
                if keys:
                    ch.enter(i, PER)
                    ch.base = i * PER
                    wait(pool, c_top, i, 1)
                    wait(pool, c_dec, i - 1, 1)
                    pool.sem_inc(pool_gates, 1)
                    tt = nc.gpsimd.tensor_tensor
                    ch.link(tt(sel[:, :, :, :], hit[:, :, :, :],
                               pay[:, :, :].unsqueeze(3).broadcast_to([P, PH, CAND, TOP]), ALU.mult))
                    n = CAND - CAND % 2
                    for w in (24, 12, 6, 3):
                        ch.link(tt(sel[:, :, 0:w, :], sel[:, :, 0:w, :], sel[:, :, w:2 * w, :], ALU.add))
                    for w in (1, 2, 48):
                        ch.link(tt(sel[:, :, 0, :], sel[:, :, 0, :], sel[:, :, w, :], ALU.add))
                    ch.link(tt(sel[:, :, 0, :], sel[:, :, 0, :], sel[:, :, 49, :], ALU.add))
                    pool.sem_inc(c_pay.sem, 1)
                    ch.n = 0
                if spread:
                    wait(pool, c_low, i - 1, 1)
                    pool.sem_inc(pool_gates, 1)
                    nc.gpsimd.tensor_tensor(B[:, 0, :, :], B[:, 0, :, :],
                                            whT[:, :].unsqueeze(1).broadcast_to([P, JJ, P]),
                                            ALU.mult).then_inc(c_high.sem, 1)

            run(pool, step)

        @block.vector
        def _(vec):
            v = nc.vector
            vec.sem_inc(c_val.sem, 1)
            vec.sem_inc(c_top.sem, 1)
            vec.sem_inc(c_dec.sem, 1)
            vec.sem_inc(c_w.sem, c_w.credit)
            ch = Chain(vec, chain)

            def weigh(i):
                wait(vec, c_e, i, 1)
                ch.link(v.tensor_reduce(den[:, :], e[:, :, :], AXX, ALU.add))
                ch.link(v.reciprocal(den[:, :], den[:, :]))
                v.tensor_tensor(wgt[:, :].rearrange("p (n k) -> p n k", n=PH), e[:, :, :],
                                den[:, :].unsqueeze(2).broadcast_to([P, PH, TOP]), ALU.mult)

            def decode(i):
                wait(vec, c_pay, i, 1)
                ch.link(v.tensor_copy(coden[:, :].rearrange("p (n k) -> p n k", n=PH), sel[:, :, 0, :]))
                v.tensor_scalar(code_r[:, :], coden[:, :], 5, None, ALU.logical_shift_right)
                ch.link(v.tensor_scalar(code_c[:, :], coden[:, :], JJ - 1, None, ALU.bitwise_and))
                v.tensor_copy(rowf[:, :], code_r[:, :])
                ch.link(v.tensor_copy(colf[:, :], code_c[:, :]))
                vec.sem_inc(c_dec.sem, 1)

            def find(i):
                wait(vec, c_S, i, 1)
                vec.sem_inc(gates, 1)
                G2 = range(2 * PH)
                for g in G2:
                    last = v.max(out=val[:, g, 0:8], in_=S[:, g, :])
                ch.link(last)
                vec.sem_inc(gates, 1)
                for g in G2:
                    v.max_index(out=idx[:, g, 0:8], in_max=val[:, g, 0:8], in_values=S[:, g, :])
                    last = v.match_replace(out=S[:, g, :], in_to_replace=val[:, g, 0:8], in_values=S[:, g, :],
                                           imm_value=LOWEST)
                ch.link(last)
                vec.sem_inc(gates, 1)
                for g in G2:
                    last = v.max(out=val[:, g, 8:16], in_=S[:, g, :])
                ch.link(last)
                vec.sem_inc(gates, 1)
                for g in G2:
                    last = v.max_index(out=idx[:, g, 8:16], in_max=val[:, g, 8:16], in_values=S[:, g, :])
                ch.link(last)
                vec.sem_inc(c_val.sem, 1)
                v.tensor_scalar(code[:, 0:PH, :], idx[:, 0:PH, :], float(JJ), None, ALU.mult)
                ch.link(v.tensor_copy(code[:, PH:, :], idx[:, PH:, :]))
                ch.link(v.tensor_scalar(over[:, :, :], code[:, PH:, :], float(JJ), float(JJ * KEYS - JJ),
                                        ALU.is_ge, ALU.mult))
                ch.link(v.tensor_tensor(code[:, PH:, :], code[:, PH:, :], over[:, :, :], ALU.add))
                wait(vec, c_pay, i - 1, 1)
                for dst, src in ((cand, val), (pay, code)):
                    for a, n, rows in ((0, 16, 1), (1, 8, 1), (2, 5, 1), (3, 4, 1), (4, 3, 1), (5, 2, 3), (8, 1, 8)):
                        o = dst[:, :, FIRST[a]:FIRST[a] + n * rows].rearrange("p h (r n) -> p h r n", n=n)
                        last = v.tensor_tensor(
                            o, src[:, 0:PH, a:a + rows].unsqueeze(3).broadcast_to([P, PH, rows, n]),
                            src[:, PH:, 0:n].unsqueeze(2).broadcast_to([P, PH, rows, n]), ALU.add)
                ch.link(last)
                vec.sem_inc(gates, 1)
                for h in range(PH):
                    last = v.max(out=best[:, h, 0:8], in_=cand[:, h, :])
                ch.link(last)
                vec.sem_inc(gates, 1)
                for h in range(PH):
                    v.max_index(out=pos[:, h, 0:8], in_max=best[:, h, 0:8], in_values=cand[:, h, :])
                    last = v.match_replace(out=left[:, h, :], in_to_replace=best[:, h, 0:8], in_values=cand[:, h, :],
                                           imm_value=LOWEST)
                ch.link(last)
                vec.sem_inc(gates, 1)
                for h in range(PH):
                    last = v.max(out=best[:, h, 8:16], in_=left[:, h, :])
                ch.link(last)
                vec.sem_inc(gates, 1)
                for h in range(PH):
                    last = v.max_index(out=pos[:, h, 8:16], in_max=best[:, h, 8:16], in_values=left[:, h, :])
                ch.link(last)
                v.tensor_tensor(e[:, :, :], best[:, :, :], best[:, :, 0:1].broadcast_to([P, PH, TOP]), ALU.subtract)
                ch.link(v.tensor_copy(pos16[:, :, :], pos[:, :, :]))
                ch.link(v.tensor_tensor(hit[:, :, :, :],
                                        pos16[:, :, :].unsqueeze(2).broadcast_to([P, PH, CAND, TOP]),
                                        m.count[:, :, :].unsqueeze(1).broadcast_to([P, PH, CAND, TOP]), ALU.is_equal))
                vec.sem_inc(c_top.sem, 1)

            def apply(i):
                wait(vec, c_g, i, NH)
                for g in range(NP):
                    wait(vec, c_p, i, g + 1)
                    part = G[:, :, g * PB:(g + 1) * PB]
                    v.tensor_tensor(part, ps_p[g % 2][:, :, :].rearrange("p t j -> p j t"), part,
                                    ALU.mult).then_inc(c_w.sem, 1)

            def spread_out(i):
                wait(vec, c_tc, i, 1)
                ch.link(v.tensor_tensor(wlT[:, :], wT[:, :], whT[:, :], ALU.subtract))
                wait(vec, c_p, i - 1, NP)
                ch.link(v.tensor_tensor(B[:, 0, :, :], colT[:, :].unsqueeze(1).broadcast_to([P, JJ, P]),
                                        m.column[:, :, :], ALU.is_equal))
                v.tensor_tensor(B[:, 1, :, :], B[:, 0, :, :], wlT[:, :].unsqueeze(1).broadcast_to([P, JJ, P]),
                                ALU.mult).then_inc(c_low.sem, 1)
                for k in range(P // JJ):
                    last = v.tensor_tensor(A[:, k * JJ:(k + 1) * JJ, :],
                                           rowT[:, k, :].unsqueeze(1).broadcast_to([P, JJ, P]),
                                           m.column[:, :, :], ALU.is_equal)
                last.then_inc(c_ab.sem, 1)

            WEIGH, FIND, DECODE, SPREAD = 2, 14, 3, 2

            def part(f, tile, base, links):
                ch.n, ch.base = 0, base
                f(tile)
                assert ch.n == links, (f, ch.n)
                return base + links

            def step(i, peeled):
                keys, spread, finish, ahead = stages(i, peeled)
                full = WEIGH + FIND + DECODE + SPREAD
                base = 0 if isinstance(i, int) and i == 0 else i * full + (FIND - full)
                if spread:
                    base = part(weigh, i - 1, base, WEIGH)
                if keys:
                    base = part(find, i, base, FIND)
                if spread:
                    base = part(decode, i - 1, base, DECODE)
                if finish:
                    apply(i - 2)
                if spread:
                    part(spread_out, i - 1, base, SPREAD)

            run(vec, step)
    t.ctx.close()


def last_combine(nc, mem, d, m):
    t = Memory(nc, mem.sems)
    H = NT // 2
    x, s, p = t.sb("fx", [P, H, C]), t.sb("fs", [P, H, C]), t.sb("fp", [P, H, C])
    x_in, gated, summed, stored = mem.sem("last_in"), mem.sem("last_gated"), mem.sem("last_summed"), mem.sem("stored")
    chain = mem.sem("last_chain")
    view = lambda a: a.rearrange("(t p) c -> p t c", p=P)
    with nc.Block() as block:
        @block.sync
        def _(sp):
            for k in range(2):
                if k:
                    sp.wait_ge(stored, 16)
                for dst, src in ((x, d["x1"]), (s, d["s1"]), (p, d["peer"])):
                    sp.dma_start(dst[:, :, :], view(src)[:, k * H:(k + 1) * H, :]).then_inc(x_in, 16)
                sp.wait_ge(summed, k + 1)
                sp.dma_start(view(d["out"])[:, k * H:(k + 1) * H, :], x[:, :, :]).then_inc(stored, 16)
            sp.wait_ge(stored, 32)

        @block.scalar
        def _(act):
            for k in range(2):
                act.wait_ge(x_in, 48 * (k + 1))
                nc.scalar.activation(p[:, :, :], p[:, :, :], ACT.Silu).then_inc(gated, 1)

        @block.vector
        def _(vec):
            ch = Chain(vec, chain)
            for k in range(2):
                vec.wait_ge(gated, k + 1)
                ch.link(nc.vector.tensor_tensor(s[:, :, :], s[:, :, :], p[:, :, :], ALU.mult))
                nc.vector.tensor_tensor(x[:, :, :], x[:, :, :], s[:, :, :], ALU.add).then_inc(summed, 1)
    t.ctx.close()


def rest(nc, mem, sems, d, m):
    layer1(nc, mem, sems, d, m)
    a = Memory(nc, sems)
    m.wk = a.sb("wk", [P, CC, 2 * PH * KEYS])
    m.down, m.up = a.sb("down", [P, CC, JJ, P]), a.sb("up", [P, JJ, C])
    m.count = a.sb("count", [P, CAND, TOP], F16)
    m.column, m.shift = a.sb("column", [P, JJ, P], F16), a.sb("shift", [P, P // JJ])
    lookup_weights(nc, mem, d, m)
    lookup_experts(nc, mem, d, m)
    a.ctx.close()
    last_combine(nc, mem, d, m)


class Names:
    pass


def build(nc, d):
    with ExitStack() as sems:
        mem = Memory(nc, sems)
        m = Names()
        m.ident, m.ones, m.eps = mem.sb("ident", [P, P]), mem.sb("ones", [P, P]), mem.sb("eps", [P, 1])
        one = Memory(nc, sems)
        m.upto, m.expert_no = one.sb("upto", [P, P]), one.sb("expert_no", [P, E])
        m.tile_start = one.sb("tile_start", [P, ET])
        m.wconv, m.affw = one.sb("wconv", [P, CC]), one.sb("affw", [P, CC, 16])
        m.aff = one.sb("aff", [P, NT, 16])
        m.tok, m.sig, m.agv = one.sb("tok", [P, NT]), one.sb("sig", [P, NT]), one.sb("agv", [P, C])
        m.place, m.tile_expert = one.sb("place", [P, NT], U32), one.sb("tile_expert", [1, ET], I32)
        m.xn = one.sb("xn", [P, NT, C])
        two = Memory(nc, sems)
        m.xh = two.sb("xh", [P, NT, C])
        three = Memory(nc, sems)
        m.xnT = three.sb("xnT", [P, CC, N])
        m.wqkv, m.wqkvT = three.sb("wqkv", [P, 3 * CC, C]), three.sb("wqkvT", [P, CC, 3 * C])
        m.l0_loads = [
            (m.wqkv[:, :, :], d["wqkv"].rearrange("(k p) c -> p k c", p=P)),
            (m.wqkvT[:, :, :], d["wqkvT"].rearrange("(k p) c -> p k c", p=P)),
            (m.wconv[:, :], d["wconv"]),
            (m.affw[:, :, 0:E], d["centT"].rearrange("(k p) e -> p k e", p=P)),
        ]
        l0_normalise(nc, mem, d, m)
        transpose_rows(nc, mem, "xn0", m.ident, m.xn, m.xnT)
        l0_global_attention(nc, mem, d, m)
        three.ctx.close()
        l0_route(nc, mem, d, m)
        two.ctx.close()
        l0_experts(nc, mem, d, m)
        l0_combine(nc, mem, d, m)
        one.ctx.close()
        rest(nc, mem, sems, d, m)
        mem.ctx.close()

SCRATCH = {"sorted_x": (ET * P, C), "sorted_y": (ET * P, C), "x1": (N, C), "xgT": (P, CC, N), "s1": (N, C),
           "peer": (N, C)}
SCRATCH16 = {"kq16": (2, 2, C, N)}


def extra_inputs(host, w, _np):
    host["gamma"] = w["L1_ffn_gamma"].reshape(CC, P).T
    host["wv"], host["wo"] = w["L1_attn_Wv"], w["L1_attn_Wo"]
    host["bv"], host["bo"] = w["L1_attn_bv"].reshape(1, C), w["L1_attn_bo"].reshape(1, C)

    host["wkq"] = _np.stack([w["L1_attn_Wk"], w["L1_attn_Wq"]])
    host["bkq"] = _np.stack([w["L1_attn_bk"], w["L1_attn_bq"]]).reshape(2, CC, P).transpose(2, 0, 1)
    f16, f32 = _np.float16, _np.float32
    slope = (_np.float32(2.0 ** (-8.0 / H)) ** _np.arange(1, H + 1, dtype=f32)).astype(f32)
    pos = _np.arange(N, dtype=f32)

    def halves(a):
        hi = a.astype(f16)
        return hi, (a - hi.astype(f32)).astype(f16)

    sh, sl = halves(slope)
    again = _np.arange(H + 2) % H
    host["slopes"] = _np.broadcast_to(_np.stack([sh, sl], 1)[again], (P, H + 2, 2))
    start = (slope[:, None] * (_np.arange(NQ) * QB) / MSCALE).astype(f32)[again]
    host["start"] = _np.broadcast_to(start, (P, H + 2, NQ))
    rel = (_np.arange(GK * NQ) - GK * (NQ - 1)) * (GK * P)
    host["abias"] = (slope[None, :, None] * (_np.arange(P)[:, None, None] + rel[None, None, :])).astype(f32)
    kspec = _np.zeros((H, NSPEC, N), f16)
    kspec[:, 0:2] = MSCALE
    kspec[:, 2:4] = (P * ((pos // P) % GK)).astype(f16)
    kspec[:, 4], kspec[:, 5] = halves(slope[:, None] * pos[None, :])
    host["kspec"] = kspec
    qspec = _np.zeros((NSPEC, N), f16)
    qspec[4:6] = 1.0
    host["qspec"] = qspec
    host["ident16"] = _np.eye(P, dtype=f16)
    pick = _np.zeros((2, GK, 32, 2, HD + 1), f32)
    for h in range(2):
        for r in range(HD + 1):
            pick[h, :, r, h, r] = 1.0
    host["pick"] = pick.reshape(P, 2 * (HD + 1))
    host["pwq"] = w["L1_ffn_wq"]
    host["keysT"] = w["L1_ffn_keys"].transpose(3, 2, 0, 1).reshape(P, 2 * PH, KEYS)
    def by_tile(a):
        return a[:TABLE_ROWS].reshape(KEYS, 2, JJ, C).transpose(2, 1, 0, 3).reshape(JJ, P, C)

    down = by_tile(w["L1_ffn_table_down"])
    host["down"] = down.reshape(JJ, P, CC, P).transpose(3, 2, 0, 1)
    host["up"] = by_tile(w["L1_ffn_table_up"]).transpose(1, 0, 2)
    host["count"] = _np.broadcast_to(_np.arange(CAND, dtype=f16)[None, :, None], (P, CAND, TOP))
    host["column"] = _np.broadcast_to(_np.arange(JJ, dtype=f16)[None, :, None], (P, JJ, P))
    host["shift"] = _np.broadcast_to(-JJ * _np.arange(P // JJ, dtype=f32), (P, P // JJ))


def kernel(**inputs):
    import numpy as _np
    import concourse.bacc as _bacc
    from concourse import mybir as _mybir
    from concourse.bass_utils import run_bass_kernel_spmd as _run

    w = {k: _np.asarray(v) for k, v in inputs.items()}
    e, f, c = w["L0_ffn_w1"].shape

    def columns(a):
        return _np.moveaxis(a.reshape(a.shape[:-1] + (a.shape[-1] // P, P)), -1, 0)

    table = _np.concatenate([columns(w[k]) for k in ("L0_ffn_ln_g", "L0_ffn_ln_b", "L0_ffn_b1")], axis=2)
    host = {
        "x": w["L0_attn_x"].reshape(N, C),
        "wqkv": w["L0_attn_w_qkv"], "wqkvT": w["L0_attn_w_qkv"].T,
        "wconv": columns(w["L0_attn_w_conv1"]),
        "centT": w["L0_ffn_centroids"].T,
        "table": table.transpose(1, 0, 2),
        "w1": w["L0_ffn_w1"].reshape(e, f, CC, P).transpose(0, 3, 2, 1),
        "w2": w["L0_ffn_w2"].reshape(e, c, FC, P).transpose(0, 3, 2, 1),
        "b2": w["L0_ffn_b2"],
    }
    extra_inputs(host, w, _np)
    nc = _bacc.Bacc("TRN2", target_bir_lowering=False, num_devices=1)
    arrays, drams = {}, {}
    for name, a in host.items():
        a = _np.ascontiguousarray(a)
        arrays[f"in_{name}"] = a
        drams[name] = nc.dram_tensor(f"in_{name}", a.shape, _mybir.dt.from_np(a.dtype), kind="ExternalInput").ap()
    drams["out"] = nc.dram_tensor("out", (N, C), F32, kind="ExternalOutput").ap()
    for name, shape in SCRATCH.items():
        drams[name] = nc.dram_tensor(name, shape, F32, kind="Internal").ap()
    for name, shape in SCRATCH16.items():
        drams[name] = nc.dram_tensor(name, shape, F16, kind="Internal").ap()
    build(nc, drams)
    r = _run(nc, [arrays], core_ids=[0])
    return r.results[0]["out"].reshape(1, N, C)
```
